# Optimizing a Trainium2 kernel written in Bass

```python
import numpy as np
import jax
import jax.numpy as jnp

def _softmax(x, axis=-1):
    return jax.nn.softmax(x, axis=axis)

def _gelu(x):
    return jax.nn.gelu(x, approximate=True)

def _silu(x):
    return jax.nn.silu(x)

def _sigmoid(x):
    return jax.nn.sigmoid(x)

def _layernorm(x, axis=-1, eps=1e-05):
    m = jnp.mean(x, axis=axis, keepdims=True)
    v = jnp.var(x, axis=axis, keepdims=True)
    return (x - m) / jnp.sqrt(v + eps)

def _scatter_add(tgt, idx, src, axis=0):
    return tgt.at[idx].add(src)

def _segment_sum(src, seg, n):
    return jax.ops.segment_sum(src, seg, n)
kernel_name = 'mk_gnn_resnorm_d1_gnn_r64_535133'

def setup_inputs(seed: int=0):
    np.random.seed(seed)
    _w = jnp.asarray

    def _rec_inputs():
        import jax
        import jax.numpy as jnp
        _gk = jax.random.key(seed)
        x = -0.0002117 + 1 * jax.random.normal(jax.random.fold_in(_gk, 1), (100000, 256), jnp.float32)
        src = jax.random.randint(jax.random.fold_in(_gk, 2), (25000,), 0, 100000, jnp.int32)
        dst = jax.random.randint(jax.random.fold_in(_gk, 3), (25000,), 0, 100000, jnp.int32)
        _o = jnp.argsort(dst, stable=True)
        src = src[_o]
        dst = dst[_o]
        return (x, src, dst)
    x, src, dst = _rec_inputs()

    def _L0_gnn_setup():
        import jax, jax.numpy as jnp
        import numpy as np
        N_NODES = 100000
        N_EDGES = 25000
        D_FEAT = 256
        HIDDEN = 256
        OUT = 256

        def _glorot(key, shape):
            fan_in, fan_out = shape
            lim = np.sqrt(6.0 / (fan_in + fan_out))
            return jax.random.uniform(key, shape, jnp.float32, -lim, lim)

        def _sage_conv(x, src, dst, W_l, b_l, W_r):
            msgs = x[src]
            agg = jax.ops.segment_sum(msgs, dst, num_segments=N_NODES)
            deg = jax.ops.segment_sum(jnp.ones((src.shape[0],), x.dtype), dst, num_segments=N_NODES)
            mean = agg / jnp.maximum(deg, 1.0)[:, None]
            return mean @ W_l + b_l + x @ W_r
        key = jax.random.key(seed)
        ks = jax.random.split(key, 8)
        x = jax.random.normal(ks[0], (N_NODES, D_FEAT), jnp.float32)
        edge_index = jax.random.randint(ks[1], (2, N_EDGES), 0, N_NODES, jnp.int64)
        return {'x': x, 'edge_index': edge_index, 'W1_l': _glorot(ks[2], (D_FEAT, HIDDEN)), 'b1': jnp.zeros((HIDDEN,), jnp.float32), 'W1_r': _glorot(ks[3], (D_FEAT, HIDDEN)), 'W2_l': _glorot(ks[4], (HIDDEN, HIDDEN)), 'b2': jnp.zeros((HIDDEN,), jnp.float32), 'W2_r': _glorot(ks[5], (HIDDEN, HIDDEN)), 'W3': _glorot(ks[6], (HIDDEN, OUT)), 'b3': jnp.zeros((OUT,), jnp.float32)}
    _L0_gnn_all = _L0_gnn_setup()
    _L0_gnn_in = {k: v for k, v in _L0_gnn_all.items() if k in ('W1_l', 'b1', 'W1_r', 'W2_l', 'b2', 'W2_r', 'W3', 'b3')}
    del _L0_gnn_all
    return {'x': x, 'src': src, 'dst': dst, 'L0_gnn_W1_l': _L0_gnn_in['W1_l'], 'L0_gnn_b1': _L0_gnn_in['b1'], 'L0_gnn_W1_r': _L0_gnn_in['W1_r'], 'L0_gnn_W2_l': _L0_gnn_in['W2_l'], 'L0_gnn_b2': _L0_gnn_in['b2'], 'L0_gnn_W2_r': _L0_gnn_in['W2_r'], 'L0_gnn_W3': _L0_gnn_in['W3'], 'L0_gnn_b3': _L0_gnn_in['b3']}

def reference(x, src, dst, L0_gnn_W1_l, L0_gnn_b1, L0_gnn_W1_r, L0_gnn_W2_l, L0_gnn_b2, L0_gnn_W2_r, L0_gnn_W3, L0_gnn_b3):
    import jax
    import jax.numpy as jnp

    def _L0_gnn_ref(x, edge_index, W1_l, b1, W1_r, W2_l, b2, W2_r, W3, b3):
        import jax, jax.numpy as jnp
        import numpy as np
        N_NODES = 100000
        N_EDGES = 25000
        D_FEAT = 256
        HIDDEN = 256
        OUT = 256

        def _glorot(key, shape):
            fan_in, fan_out = shape
            lim = np.sqrt(6.0 / (fan_in + fan_out))
            return jax.random.uniform(key, shape, jnp.float32, -lim, lim)

        def _sage_conv(x, src, dst, W_l, b_l, W_r):
            msgs = x[src]
            agg = jax.ops.segment_sum(msgs, dst, num_segments=N_NODES)
            deg = jax.ops.segment_sum(jnp.ones((src.shape[0],), x.dtype), dst, num_segments=N_NODES)
            mean = agg / jnp.maximum(deg, 1.0)[:, None]
            return mean @ W_l + b_l + x @ W_r
        src, dst = (edge_index[0], edge_index[1])
        h = jax.nn.relu(_sage_conv(x, src, dst, W1_l, b1, W1_r))
        h = jax.nn.relu(_sage_conv(h, src, dst, W2_l, b2, W2_r))
        return h @ W3 + b3
    edge_index = jnp.stack([src, dst])
    x = _layernorm(x + _L0_gnn_ref(x, edge_index, L0_gnn_W1_l, L0_gnn_b1, L0_gnn_W1_r, L0_gnn_W2_l, L0_gnn_b2, L0_gnn_W2_r, L0_gnn_W3, L0_gnn_b3), axis=-1)
    return x

_drawn_inputs = setup_inputs


def setup_inputs(seed=0):
    import zlib

    import numpy as np

    out = dict(_drawn_inputs(seed))
    spreads = {'L0_gnn_b1': (0.0, 0.1), 'L0_gnn_b2': (0.0, 0.1), 'L0_gnn_b3': (0.0, 0.1)}
    factors = {}
    for name, (base, spread) in spreads.items():
        noise = np.random.default_rng([zlib.crc32(name.encode()), seed]).standard_normal(out[name].shape)
        drawn = base * np.exp(spread * noise) if base else spread * noise
        out[name] = jnp.asarray(drawn.astype(out[name].dtype))
    for name, factor in factors.items():
        out[name] = (out[name] * factor).astype(out[name].dtype)
    return out
```

```python
from contextlib import ExitStack

import concourse.bass as bass
from concourse import mybir

P = 128
S = 4
G = S * P
U = 4
EPS = 1e-5
FAR = 1 << 20


def build(nc, x, src, dst, W1_l, b1, W1_r, W2_l, b2, W2_r, W3, b3, out):
    f32, f32r, i32 = mybir.dt.float32, mybir.dt.float32r, mybir.dt.int32
    ALU, ACT = mybir.AluOpType, mybir.ActivationFunctionType
    N, D = x.shape
    E = src.shape[0]
    K = D // P
    NG = -(-N // G)
    NI = NG // U
    NE = -(-E // G)
    EP = NE * G
    NT = EP // P
    Q = EP // 256
    QF, QR = E // 256, E % 256
    assert NG == NI * U and NE == NI and NT == 2 * Q and N < FAR and QF == Q - 1 and D == 256
    HALF = NE
    MIDDLE = HALF // 2
    X1R, X2R, X3, X1L, X2L = range(5)

    with ExitStack() as ctx:
        def sb(name, shape, dt=f32):
            return ctx.enter_context(nc.sbuf_tensor(name, shape, dt))

        def pb(name):
            return ctx.enter_context(nc.psum_tensor(name, [P, K, G], f32))

        def sem(name):
            return ctx.enter_context(nc.semaphore(name))

        h_tab = nc.dram_tensor("h_tab", [2 * EP, D], f32, kind="Internal").ap()
        xdb_tab = nc.dram_tensor("xdb_tab", [EP, D], f32, kind="Internal").ap()
        slot_tab = nc.dram_tensor("slot_tab", [N, 1], i32, kind="Internal").ap()
        seg_tab = nc.dram_tensor("seg_tab", [NE, 2, G], f32, kind="Internal").ap()

        ident = sb("ident", [P, P])
        w_raw = sb("w_raw", [P, 5, K, D])
        w_hi = sb("w_hi", [P, 5, K, D], f32r)
        w_lo = sb("w_lo", [P, 5, K, D], f32r)
        bias = sb("bias", [P, 2, K])
        b3_row = sb("b3_row", [P, D])
        eps = sb("eps", [P, 1])
        xn = sb("xn", [P, U, S, D])
        xb = sb("xb", [P, 2, S, D])
        xt_hi = sb("xt_hi", [P, 2, K, G], f32r)
        xt_lo = sb("xt_lo", [P, 2, K, G], f32r)
        h_full = sb("h_full", [P, 2, K, G])
        h_hi = sb("h_hi", [P, 2, K, G], f32r)
        h_lo = sb("h_lo", [P, 2, K, G], f32r)
        y = sb("y", [P, 2, S, D])
        o = sb("o", [P, 2, S, D])
        stats = sb("stats", [P, S, 6])
        mv = sb("mv", [P, 2, S, 2])
        sd = sb("sd", [P, 2, S])
        rs = sb("rs", [P, 2, S])
        nb = sb("nb", [P, 2, S])
        xe = sb("xe", [P, 2, S, D])
        xe_hi = sb("xe_hi", [P, 2, K, G], f32r)
        xe_lo = sb("xe_lo", [P, 2, K, G], f32r)
        seg = sb("seg", [P, 2, G])
        run = sb("run", [P, K, G])
        mean = sb("mean", [P, K, G])
        mean_hi = sb("mean_hi", [P, K, G], f32r)
        mean_lo = sb("mean_lo", [P, K, G], f32r)
        src_h = sb("src_h", [P, S, D])
        dst_h = sb("dst_h", [P, S, D])
        xdb = sb("xdb", [P, S, D])
        idx = sb("idx", [P, 3, NT], i32)
        own = sb("own", [P, NT], i32)
        base = sb("base", [P, NT], i32)
        slots = sb("slots", [P, NT], i32)
        h_row = sb("h_row", [P, NT], i32)
        e_stage = sb("e_stage", [P, 2, S], i32)
        t_stage = sb("t_stage", [P, 3, S], i32)
        c_stage = sb("c_stage", [P, 2, 2, S], i32)
        ps_x, ps_h1, ps_h2, ps_y = pb("ps_x"), pb("ps_h1"), pb("ps_h2"), pb("ps_y")
        ps_h = [ps_h1, ps_h2]

        pre = h_full[:, :, :, :].rearrange("p a k g -> p (a k g)")
        e_int = pre[0:Q, 0:1024].bitcast(i32).rearrange("p (a j) -> p a j", a=4)
        fill = pre[:, 1024:1824].bitcast(i32)
        e_f = y[:, :, :, :].rearrange("p a s d -> p (a s) d")[:, 0:4]
        p_src, p_dst, p_prev, p_next = (e_f[0:Q, n] for n in range(4))
        e_w = y[:, :, :, :].rearrange("p a s d -> p (a s) d")
        same, seg_last, count, whole = (e_w[0:Q, n] for n in range(4, 8))
        e_idx = o[:, :, :, :].rearrange("p a s d -> p (a s) d")[:, 0:3]
        tr = o[:, :, :, :].rearrange("p a s d -> p (a s d)")[:, 768:1152].rearrange("p (n c) -> p n c", n=3)
        ones = o[:, :, :, :].rearrange("p a s d -> p (a s d)")[:, 1152:1408]
        rdeg = o[:, :, :, :].rearrange("p a s d -> p (a s d)")[:, 1408:1664]
        rows3 = o[:, :, :, :].rearrange("p a s d -> p (a s d)")[:, 1664:2048].rearrange("p (n c) -> p n c", n=3)

        w_in, b_in, made, cleared, e_in = (sem(n) for n in ("w_in", "b_in", "made", "cleared", "e_in"))
        w_hi_ok, w_ok, prep, turned_pre, idx_ok = (sem(n) for n in ("w_hi_ok", "w_ok", "prep", "turned_pre", "idx_ok"))
        seg_out, fill_out = sem("seg_out"), sem("fill_out")
        x_in = [sem(f"x_in{u}") for u in range(U)]
        y_out = [sem(f"y_out{b}") for b in range(2)]
        xt_ps, xhi_ok, xlo_ok = sem("xt_ps"), sem("xhi_ok"), sem("xlo_ok")
        l_ps = [sem("l1_ps"), sem("l2_ps")]
        l3_ps = sem("l3_ps")
        hf_ok = [sem("h1f_ok"), sem("h2f_ok")]
        hhi_ok = [sem("h1hi_ok"), sem("h2hi_ok")]
        hlo_ok = [sem("h1lo_ok"), sem("h2lo_ok")]
        xb_ok, y_ok, stastage_ok, mv_ok, sd_ok, rs_ok, nb_ok, o_ok = (sem(n) for n in (
            "xb_ok", "y_ok", "stastage_ok", "mv_ok", "sd_ok", "rs_ok", "nb_ok", "o_ok"))
        xs_in, xd_in, seg_in = sem("xs_in"), sem("xd_in"), sem("seg_in")
        xs_ps, xd_ps, src_ps, dst_ps = sem("xs_ps"), sem("xd_ps"), sem("src_ps"), sem("dst_ps")
        xshi_ok, xdhi_ok, mhi_ok = sem("xshi_ok"), sem("xdhi_ok"), sem("mhi_ok")
        run_ok, mean_ok, xs_ok, xd_ok, mlo_ok = (sem(n) for n in ("run_ok", "mean_ok", "xs_ok", "xd_ok", "mlo_ok"))
        src_ok, dst_ok, xdb_ok = sem("src_ok"), sem("dst_ok"), sem("xdb_ok")
        src_out, dst_out, xdb_out = sem("src_out"), sem("dst_out"), sem("xdb_out")
        stage_ok, tab_out, slot_in, slots_ok = (sem(n) for n in ("stage_ok", "tab_out", "slot_in", "slots_ok"))
        row_ok = sem("row_ok")
        c_hs_in = [sem(f"c_hs_in{b}") for b in range(2)]
        c_hd_in = [sem(f"c_hd_in{b}") for b in range(2)]
        c_xb_in = [sem(f"c_xb_in{b}") for b in range(2)]
        c_seg_in = [sem(f"c_seg_in{b}") for b in range(2)]
        c_out = [sem(f"c_out{b}") for b in range(2)]
        c_hs_ps, c_hd_ps, c_l2_ps, c_l3_ps = (sem(n) for n in (
            "c_hs_ps", "c_hd_ps", "c_l2_ps", "c_l3_ps"))
        c_hs_ok, c_hdf_ok, c_hdhi_ok, c_hdlo_ok, c_run_ok, c_mean_ok, c_mhi_ok, c_mlo_ok = (sem(n) for n in (
            "c_hs_ok", "c_hdf_ok", "c_hdhi_ok", "c_hdlo_ok", "c_run_ok", "c_mean_ok", "c_mhi_ok", "c_mlo_ok"))
        c_hf_ok, c_hhi_ok, c_hlo_ok, c_y_ok, c_stastage_ok, c_mv_ok, c_sd_ok, c_rs_ok, c_nb_ok, c_o_ok = (sem(n) for n in (
            "c_hf_ok", "c_hhi_ok", "c_hlo_ok", "c_y_ok", "c_stastage_ok", "c_mv_ok", "c_sd_ok", "c_rs_ok", "c_nb_ok", "c_o_ok"))

        def after(eng, s, value):
            if not (isinstance(value, int) and value <= 0):
                eng.wait_ge(s, value)

        def rows(t, g):
            first = min(g * G, N - G) if isinstance(g, int) else g * G
            return t[bass.ds(first, G), :].rearrange("(p s) d -> p s d", s=S)

        def slots_of(t, j, start=0):
            first = j * G + start
            return t[bass.ds(first, G), :].rearrange("(s p) d -> p s d", p=P)

        def passes(eng, body):
            body(0, True, False)
            with eng.Fori(1, NI - 1) as i:
                body(i, False, False)
            body(NI - 1, False, True)

        def edge_passes(eng, step):
            for j in range(3):
                step(j, j % 2, False)
            with eng.Fori(0, (NE - 5) // 2) as m:
                step(m * 2 + 3, 1, False)
                step(m * 2 + 4, 0, False)
            step(NE - 2, 1, False)
            step(NE - 1, 0, True)

        def slot_use(j, parity, n=16):
            return n * ((j - parity) // 2 + 1) if isinstance(j, int) else (j - parity + 2) * (n // 2)

        def seg_of(b):
            return (seg[:, :, :].rearrange("p a g -> p (a g)"), src_h[:, :, :].rearrange("p s d -> p (s d)"))[b]

        hd_full = dst_h[:, :, :].rearrange("p (k a) d -> p k (a d)", k=K)

        block = ctx.enter_context(nc.Block())

        @block.sync
        def _(sp):
            for n, w in enumerate((W1_r, W2_r, W3, W1_l, W2_l)):
                sp.dma_start(w_raw[:, n], w.rearrange("(k p) n -> p k n", p=P)).then_inc(w_in, 16)
            for n, b in enumerate((b1, b2)):
                for k in range(K):
                    sp.dma_start(bias[:, n, k:k + 1], b[k * P:(k + 1) * P].rearrange("(p a) -> p a", a=1)).then_inc(b_in, 16)
            sp.dma_start(b3_row[:, :], b3.rearrange("(a n) -> a n", a=1).to_broadcast([P, D])).then_inc(b_in, 16)
            for u in range(U):
                sp.dma_start(xn[:, u], rows(x, u)).then_inc(x_in[u], 16)
            sp.wait_ge(cleared, 4)
            sp.dma_start(slot_tab.rearrange("(p c) a -> p (c a)", p=125), fill[0:125, :]).then_inc(fill_out, 16)
            sp.wait_ge(prep, PREP_RDEG)
            for h in range(2):
                sp.dma_start(seg_tab[:, 0, h * 256:(h + 1) * 256], same[h:Q:2, :]).then_inc(seg_out, 16)
                sp.dma_start(seg_tab[:, 1, h * 256:(h + 1) * 256], rdeg[h:Q:2, :]).then_inc(seg_out, 16)
            sp.wait_ge(seg_out, 64)

            def store(g, b):
                sp.wait_ge(o_ok, g + 1)
                sp.dma_start(rows(out, g), o[:, b]).then_inc(y_out[b], 16)

            def body(i, first, last):
                for u in range(U):
                    g = i * U + u
                    if not first:
                        sp.wait_ge(xt_ps, (g - U + 1) * K)
                        sp.wait_ge(xb_ok, g - U + 1)
                        sp.dma_start(xn[:, u], rows(x, g)).then_inc(x_in[u], 16)
                    if u == 0:
                        after(sp, mean_ok, i)
                        sp.dma_start(seg[:, :, :].rearrange("p a g -> p (a g)"),
                                     seg_tab[bass.ds(i, 1), :, :].rearrange("j a g -> j (a g)").to_broadcast([P, 2 * G]))\
                            .then_inc(seg_in, 16)
                    if not first:
                        store(g - U, u % 2)
            passes(sp, body)
            for g in range(NG - U, NG):
                if g == NG - 1:
                    sp.wait_ge(y_out[(g - 1) % 2], 16 * (NG // 2))
                store(g, g % 2)

            sp.wait_ge(dst_out, 16 * NE)
            sp.wait_ge(src_out, 16 * NE)
            sp.wait_ge(xdb_out, 16 * NE)
            sp.wait_ge(mean_ok, NI)
            sp.wait_ge(xb_ok, NG)
            sp.wait_ge(xt_ps, NG * K)
            sp.wait_ge(y_ok, NG * K)

            def load(j, b):
                after(sp, c_hd_ps, (j - 1) * K)
                sp.dma_start(xn[:, 2 + b], slots_of(h_tab, j)).then_inc(c_hd_in[b], 16)
                after(sp, c_mean_ok, j - 1)
                sp.dma_start(seg_of(b), seg_tab[bass.ds(j, 1), :, :].rearrange("j a g -> j (a g)").to_broadcast([P, 2 * G]))\
                    .then_inc(c_seg_in[b], 16)
                after(sp, c_y_ok, (j - 1) * K)
                sp.dma_start(xb[:, b], slots_of(xdb_tab, j)).then_inc(c_xb_in[b], 16)

            load(0, 0)

            def step(j, b, last):
                if not last:
                    load(j + 1, 1 - b)
            edge_passes(sp, step)

        @block.gpsimd
        def _(pool):
            staged = pool.alloc_register("staged")
            pool.reg_mov(staged, 1)

            def wait_staged():
                pool.wait_ge(stage_ok, pool.snap(staged, min_val=1, max_val=10 * NE))
                pool.reg_add(staged, staged, 1)

            nc.gpsimd.memset(e_int[:, 0], 0).then_inc(made, 1)
            nc.gpsimd.memset(e_int[:, 1:4], N).then_inc(made, 1)
            pool.wait_ge(made, 2)
            nc.gpsimd.memset(e_int[0:1, 2, 0:1], -1).then_inc(cleared, 1)
            nc.gpsimd.memset(fill, FAR).then_inc(cleared, 1)
            nc.gpsimd.memset(e_idx, 0.0).then_inc(cleared, 1)
            nc.gpsimd.memset(tr, 0.0).then_inc(cleared, 1)
            nc.gpsimd.memset(ones, 1.0).then_inc(cleared, 1)
            nc.gpsimd.memset(run[:, :, :], 0.0).then_inc(cleared, 1)
            nc.gpsimd.memset(eps[:, :], EPS).then_inc(cleared, 1)
            nc.gpsimd.memset(ident[:, :], 0.0).then_inc(made, 1)
            pool.wait_ge(made, 3)
            nc.gpsimd.affine_select(out=ident[:, :], in_=ident[:, :], compare_op=ALU.not_equal, fill=1.0,
                                    base=0, pattern=[[-1, P]], channel_multiplier=1).then_inc(cleared, 1)
            nc.gpsimd.iota(own[:, :], [[P, NT]], base=0, channel_multiplier=1).then_inc(cleared, 1)
            nc.gpsimd.iota(base[:, :], [[P, NT]], base=EP, channel_multiplier=1).then_inc(cleared, 1)
            pool.wait_ge(cleared, 10)
            pool.wait_ge(idx_ok, 6)
            pool.wait_ge(fill_out, 16)
            pool.wait_ge(b_in, 80)

            def gather(i, kind, ps, landed):
                after(pool, landed, 16 * S * i)
                after(pool, ps, i * K)
                if kind == 1:
                    after(pool, xdb_ok, i)
                nc.gpsimd.tensor_copy(e_stage[:, kind], idx[:, kind, bass.ds(i * S, S)]).then_inc(stage_ok, 1)
                wait_staged()
                for s in range(S):
                    nc.gpsimd.indirect_dma_start(
                        out=xe[:, kind, s], out_offset=None, in_=x,
                        in_offset=bass.IndirectOffsetOnAxis(ap=e_stage[:, kind, s:s + 1], axis=0)).then_inc(landed, 16)

            def note_slots(n):
                after(pool, tab_out, 16 * S * n)
                nc.gpsimd.tensor_copy(t_stage[:, 0], idx[:, 2, bass.ds(n * S, S)])
                nc.gpsimd.tensor_copy(t_stage[:, 1], own[:, bass.ds(n * S, S)]).then_inc(stage_ok, 1)
                wait_staged()
                for s in range(S):
                    nc.gpsimd.indirect_dma_start(
                        out=slot_tab, out_offset=bass.IndirectOffsetOnAxis(ap=t_stage[:, 0, s:s + 1], axis=0),
                        in_=t_stage[:, 1, s:s + 1], in_offset=None, bounds_check=N - 1, oob_is_err=False).then_inc(tab_out, 16)

            def keep_slots(m):
                pool.wait_ge(slot_in, 16 * S * (m + 1))
                nc.gpsimd.tensor_copy(slots[:, bass.ds(m * S, S)], t_stage[:, 2]).then_inc(slots_ok, 1)

            def look_up(m):
                if isinstance(m, int) and m == 0:
                    pool.wait_ge(tab_out, 16 * S * NE)
                else:
                    keep_slots(m - 1)
                after(pool, slots_ok, m)
                nc.gpsimd.tensor_copy(t_stage[:, 0], idx[:, 0, bass.ds(m * S, S)]).then_inc(stage_ok, 1)
                wait_staged()
                for s in range(S):
                    nc.gpsimd.indirect_dma_start(
                        out=t_stage[:, 2, s:s + 1], out_offset=None, in_=slot_tab,
                        in_offset=bass.IndirectOffsetOnAxis(ap=t_stage[:, 0, s:s + 1], axis=0)).then_inc(slot_in, 16)

            def batch(i, half, phase):
                if phase == 0 or (phase == 1 and half == 0):
                    note_slots(i * 2 + half)
                else:
                    look_up(i * 2 + half - HALF)

            def normalise(b):
                for s in range(S):
                    ins = nc.gpsimd.tensor_scalar(o[:, b, s], y[:, b, s], rs[:, b, s:s + 1], nb[:, b, s:s + 1], ALU.mult, ALU.add)
                ins.then_inc(o_ok, 1)

            def body(i, first, last, phase):
                for u in range(U):
                    g = i * U + u
                    b = u % 2
                    after(pool, nb_ok, g)
                    if not (first and u < 3):
                        pool.wait_ge(y_out[1 - b], 8 * (g - 2 + b))
                    pool.wait_ge(x_in[u], 16 * (i + 1))
                    after(pool, y_ok, (g - 1) * K)
                    nc.gpsimd.tensor_tensor(xb[:, b], xn[:, u],
                                            b3_row[:, :].unsqueeze(1).to_broadcast([P, S, D]), ALU.add).then_inc(xb_ok, 1)
                    if not (first and u == 0):
                        normalise(1 - b)
                    if u == 0:
                        pool.wait_ge(xd_in, 16 * S * (i + 1))
                        after(pool, xdb_out, 16 * i)
                        nc.gpsimd.tensor_tensor(xdb[:, :, :], xe[:, 1],
                                                b3_row[:, :].unsqueeze(1).to_broadcast([P, S, D]), ALU.add).then_inc(xdb_ok, 1)
                        batch(i, 0, phase)
                    if u == 1 and not last:
                        gather(i + 1, 0, xs_ps, xs_in)
                    if u == 2 and not last:
                        gather(i + 1, 1, xd_ps, xd_in)
                    if u == 3:
                        batch(i, 1, phase)

            gather(0, 0, xs_ps, xs_in)
            gather(0, 1, xd_ps, xd_in)
            body(0, True, False, 0)
            with pool.Fori(1, MIDDLE) as i:
                body(i, False, False, 0)
            body(MIDDLE, False, False, 1)
            with pool.Fori(MIDDLE + 1, NI - 1) as i:
                body(i, False, False, 2)
            body(NI - 1, False, True, 2)
            keep_slots(NE - 1)
            pool.wait_ge(nb_ok, NG)
            pool.wait_ge(y_out[1], 16 * (NG // 2 - 1))
            normalise(1)

            pool.wait_ge(row_ok, 1)
            pool.wait_ge(src_out, 16 * NE)
            pool.wait_ge(dst_out, 16 * NE)
            pool.wait_ge(xt_ps, NG * K)
            for b in range(2):
                pool.wait_ge(y_out[b], 16 * (NG // 2))

            def fetch(j, b):
                after(pool, c_hs_in[b], 0 if isinstance(j, int) and j < 2 else slot_use(j - 2, b, 16 * S))
                after(pool, c_hs_ps, (j - 1) * K)
                nc.gpsimd.tensor_copy(c_stage[:, b, 0], h_row[:, bass.ds(j * S, S)]).then_inc(stage_ok, 1)
                wait_staged()
                for s in range(S):
                    nc.gpsimd.indirect_dma_start(
                        out=xn[:, b, s], out_offset=None, in_=h_tab,
                        in_offset=bass.IndirectOffsetOnAxis(ap=c_stage[:, b, 0, s:s + 1], axis=0)).then_inc(c_hs_in[b], 16)

            def scatter(j, b):
                after(pool, c_out[b], 0 if isinstance(j, int) and j < 2 else slot_use(j - 2, b, 16 * S))
                nc.gpsimd.tensor_copy(c_stage[:, b, 1], idx[:, 2, bass.ds(j * S, S)]).then_inc(stage_ok, 1)
                wait_staged()
                pool.wait_ge(c_o_ok, pool.snap(scattered, min_val=1, max_val=NE))
                pool.reg_add(scattered, scattered, 1)
                for s in range(S):
                    nc.gpsimd.indirect_dma_start(
                        out=out, out_offset=bass.IndirectOffsetOnAxis(ap=c_stage[:, b, 1, s:s + 1], axis=0),
                        in_=o[:, b, s], in_offset=None, bounds_check=N - 1, oob_is_err=False).then_inc(c_out[b], 16)

            scattered = pool.alloc_register("scattered")
            pool.reg_mov(scattered, 1)
            fetch(0, 0)

            def step(j, b, last):
                if not last:
                    fetch(j + 1, 1 - b)
                if not (isinstance(j, int) and j == 0):
                    scatter(j - 1, 1 - b)
                if last:
                    scatter(j, b)
            edge_passes(pool, step)
            pool.wait_ge(stage_ok, pool.snap(staged) - 1)
            pool.wait_ge(c_o_ok, pool.snap(scattered) - 1)
            pool.wait_ge(c_out[0], 16 * S * (NE // 2 + 1))
            pool.wait_ge(c_out[1], 16 * S * (NE // 2))

        @block.scalar
        def _(act):
            act.wait_ge(cleared, 1)
            FULL = QF * 256
            act.dma_start(e_int[0:QF, 0], src[0:FULL].rearrange("(q j) -> q j", j=256)).then_inc(e_in, 16)
            act.dma_start(e_int[QF:Q, 0, 0:QR], src[FULL:E].rearrange("(a j) -> a j", a=1)).then_inc(e_in, 16)
            act.dma_start(e_int[0:QF, 1], dst[0:FULL].rearrange("(q j) -> q j", j=256)).then_inc(e_in, 16)
            act.dma_start(e_int[QF:Q, 1, 0:QR], dst[FULL:E].rearrange("(a j) -> a j", a=1)).then_inc(e_in, 16)
            act.dma_start(e_int[0:1, 2, 1:256], dst[0:255].rearrange("(a j) -> a j", a=1)).then_inc(e_in, 16)
            act.dma_start(e_int[1:QF, 2], dst[255:FULL - 1].rearrange("(q j) -> q j", j=256)).then_inc(e_in, 16)
            act.dma_start(e_int[QF:Q, 2, 0:QR + 1], dst[FULL - 1:E].rearrange("(a j) -> a j", a=1)).then_inc(e_in, 16)
            act.dma_start(e_int[0:QF, 3], dst[1:FULL + 1].rearrange("(q j) -> q j", j=256)).then_inc(e_in, 16)
            act.dma_start(e_int[QF:Q, 3, 0:QR - 1], dst[FULL + 1:E].rearrange("(a j) -> a j", a=1)).then_inc(e_in, 16)
            act.wait_ge(w_in, 80)
            nc.scalar.copy(w_hi[:, :, :, :], w_raw[:, :, :, :]).then_inc(w_hi_ok, 1)
            act.wait_ge(b_in, 80)
            act.wait_ge(cleared, 8)
            act.wait_ge(prep, PREP_END)

            def evac_x(g, b):
                for k in range(K):
                    act.wait_ge(xt_ps, g * K + k + 1)
                    nc.scalar.copy(xt_hi[:, b, k], ps_x[:, k]).then_inc(xhi_ok, 1)

            def evac_h(g, n):
                for k in range(K):
                    act.wait_ge(l_ps[n], g * K + k + 1)
                    nc.scalar.activation(h_full[:, n, k], ps_h[n][:, k], ACT.Relu, bias=bias[:, n, k:k + 1]).then_inc(hf_ok[n], 1)
                    act.wait_ge(hf_ok[n], g * K + k + 1)
                    nc.scalar.copy(h_hi[:, n, k], h_full[:, n, k]).then_inc(hhi_ok[n], 1)

            def deviation(g, b):
                act.wait_ge(mv_ok, g + 1)
                nc.scalar.activation(sd[:, b], mv[:, b, :, 1], ACT.Sqrt, bias=eps[:, :]).then_inc(sd_ok, 1)

            def edges(i, u):
                if u == 0:
                    for k in range(K):
                        act.wait_ge(xs_ps, i * K + k + 1)
                        nc.scalar.copy(xe_hi[:, 0, k], ps_x[:, k]).then_inc(xshi_ok, 1)
                if u == 1:
                    for k in range(K):
                        act.wait_ge(xd_ps, i * K + k + 1)
                        nc.scalar.copy(xe_hi[:, 1, k], ps_x[:, k]).then_inc(xdhi_ok, 1)
                    act.wait_ge(mean_ok, i + 1)
                    nc.scalar.copy(mean_hi[:, :, :], mean[:, :, :]).then_inc(mhi_ok, 1)
                if u == 2:
                    for k in range(K):
                        act.wait_ge(src_ps, i * K + k + 1)
                        after(act, src_out, 16 * i)
                        nc.scalar.copy(src_h[:, 2 * k:2 * k + 2].rearrange("p s d -> p (s d)"), ps_x[:, k]).then_inc(src_ok, 1)
                if u == 3:
                    for k in range(K):
                        act.wait_ge(dst_ps, i * K + k + 1)
                        after(act, dst_out, 16 * i)
                        nc.scalar.copy(dst_h[:, 2 * k:2 * k + 2].rearrange("p s d -> p (s d)"), ps_x[:, k]).then_inc(dst_ok, 1)

            def edge_stores(i, u):
                if u == 2:
                    act.wait_ge(xdb_ok, i + 1)
                    act.dma_start(slots_of(xdb_tab, i), xdb[:, :, :]).then_inc(xdb_out, 16)
                if u == 3:
                    act.wait_ge(src_ok, (i + 1) * K)
                    act.dma_start(slots_of(h_tab, i, EP), src_h[:, :, :]).then_inc(src_out, 16)
                    act.wait_ge(dst_ok, (i + 1) * K)
                    act.dma_start(slots_of(h_tab, i), dst_h[:, :, :]).then_inc(dst_out, 16)

            def body(i, first, last):
                for u in range(U):
                    g = i * U + u
                    if first and u == 0:
                        evac_x(g, 0)
                    if not (last and u == U - 1):
                        evac_x(g + 1, (u + 1) % 2)
                    evac_h(g, 0)
                    if not (first and u == 0):
                        deviation(g - 1, (u + 1) % 2)
                    edges(i, u)
                    evac_h(g, 1)
                    edge_stores(i, u)
                if last:
                    deviation(NG - 1, 1)
            passes(act, body)

            def front(j, b):
                for k in range(K):
                    act.wait_ge(c_hs_ps, j * K + k + 1)
                    nc.scalar.activation(h_full[:, 0, k], ps_x[:, k], ACT.Relu, bias=bias[:, 0, k:k + 1]).then_inc(c_hs_ok, 1)
                for k in range(K):
                    act.wait_ge(c_hd_ps, j * K + k + 1)
                    after(act, c_hdlo_ok, j * K)
                    nc.scalar.activation(hd_full[:, k], ps_h1[:, k], ACT.Relu, bias=bias[:, 0, k:k + 1]).then_inc(c_hdf_ok, 1)
                    act.wait_ge(c_hdf_ok, j * K + k + 1)
                    nc.scalar.copy(xe_hi[:, b, k], hd_full[:, k]).then_inc(c_hdhi_ok, 1)

            def mean_high(j, b):
                act.wait_ge(c_mean_ok, j + 1)
                nc.scalar.copy(xt_hi[:, b], mean[:, :, :]).then_inc(c_mhi_ok, 1)

            def second(j, b):
                for k in range(K):
                    after(act, c_hlo_ok, (j - 1) * K + k + 1)
                    act.wait_ge(c_l2_ps, j * K + k + 1)
                    nc.scalar.activation(h_full[:, 1, k], ps_h2[:, k], ACT.Relu, bias=bias[:, 1, k:k + 1]).then_inc(c_hf_ok, 1)
                    act.wait_ge(c_hf_ok, j * K + k + 1)
                    nc.scalar.copy(h_hi[:, b, k], h_full[:, 1, k]).then_inc(c_hhi_ok, 1)

            def tail(j, b):
                act.wait_ge(c_mv_ok, j + 1)
                nc.scalar.activation(sd[:, b], mv[:, b, :, 1], ACT.Sqrt, bias=eps[:, :]).then_inc(c_sd_ok, 1)
                after(act, c_out[b], 0 if isinstance(j, int) and j < 2 else slot_use(j - 2, b, 16 * S))
                act.wait_ge(c_nb_ok, j + 1)
                for s in range(S):
                    ins = nc.scalar.activation(o[:, b, s], y[:, b, s], ACT.Identity, bias=nb[:, b, s:s + 1], scale=rs[:, b, s:s + 1])
                ins.then_inc(c_o_ok, 1)

            act.wait_ge(dst_out, 16 * NE)
            act.wait_ge(o_ok, NG)
            for b in range(2):
                act.wait_ge(y_out[b], 16 * (NG // 2))
            front(0, 0)
            mean_high(0, 0)

            def step(j, b, last):
                if not last:
                    front(j + 1, 1 - b)
                second(j, b)
                if not last:
                    mean_high(j + 1, 1 - b)
                if not (isinstance(j, int) and j == 0):
                    tail(j - 1, 1 - b)
                if last:
                    tail(j, b)
            edge_passes(act, step)

        @block.vector
        def _(dve):
            done = [0]

            def link(ins):
                done[0] += 1
                ins.then_inc(prep, 1)
                dve.wait_ge(prep, done[0])

            dve.wait_ge(cleared, 7)
            dve.wait_ge(e_in, 16 * 9)
            link(nc.vector.tensor_copy(e_f[0:Q], e_int))
            link(nc.vector.tensor_tensor(same, p_dst, p_prev, ALU.is_equal))
            link(nc.vector.tensor_tensor(seg_last, p_dst, p_next, ALU.not_equal))
            link(nc.vector.tensor_tensor_scan(count, same, ones[0:Q, :], 0.0, ALU.mult, ALU.add))
            link(nc.vector.tensor_tensor_scan(whole, same, ones[0:Q, :], 1.0, ALU.mult, ALU.mult))
            link(nc.vector.tensor_copy(tr[0:Q, 0, 0:1], count[:, 255:256]))
            link(nc.vector.tensor_copy(tr[0:Q, 1, 0:1], whole[:, 255:256]))
            assert done[0] == PREP_ENDS
            dve.wait_ge(turned_pre, 1)
            link(nc.vector.tensor_copy(rows3[0:1, 0:2], ps_y[0:1, 0, 0:256].rearrange("p (n c) -> p n c", n=2)))
            link(nc.vector.tensor_tensor_scan(rows3[0:1, 2, 0:Q], rows3[0:1, 1, 0:Q], rows3[0:1, 0, 0:Q], 0.0, ALU.mult, ALU.add))
            link(nc.vector.tensor_copy(tr[0:1, 2, 1:Q], rows3[0:1, 2, 0:Q - 1]))
            assert done[0] == PREP_CARRY
            dve.wait_ge(turned_pre, 2)
            link(nc.vector.tensor_copy(rows3[:, 1, 0:1], ps_y[:, 0, 0:1]))
            link(nc.vector.scalar_tensor_tensor(count, whole, rows3[0:Q, 1, 0:1], count, ALU.mult, ALU.add))
            link(nc.vector.reciprocal(rdeg[0:Q, :], count))
            assert done[0] == PREP_RDEG
            link(nc.vector.tensor_copy(e_idx[0:Q, 0], p_src))
            link(nc.vector.tensor_scalar(e_idx[0:Q, 1], p_dst, float(N - 1), None, ALU.min))
            link(nc.vector.tensor_scalar(p_prev, p_dst, float(-FAR), None, ALU.add))
            link(nc.vector.tensor_tensor(p_next, p_prev, seg_last, ALU.mult))
            link(nc.vector.tensor_scalar(e_idx[0:Q, 2], p_next, float(FAR), None, ALU.add))
            assert done[0] == PREP_IDX
            dve.wait_ge(turned_pre, 3)
            for n in range(3):
                for h in range(2):
                    c = (2 * n + h) * P
                    nc.vector.tensor_copy(idx[:, n, h:NT:2], ps_h1[:, c // G, c % G:c % G + Q]).then_inc(idx_ok, 1)
            dve.wait_ge(w_hi_ok, 1)
            nc.vector.tensor_tensor(w_lo[:, :, :, :], w_raw[:, :, :, :], w_hi[:, :, :, :].bitcast(f32), ALU.subtract).then_inc(w_ok, 1)
            dve.wait_ge(seg_out, 64)
            dve.wait_ge(fill_out, 16)
            nc.vector.memset(stats[:, :, :], 0.0).then_inc(prep, 1)
            assert done[0] + 1 == PREP_END

            def low_x(g, b):
                for k in range(K):
                    dve.wait_ge(xhi_ok, g * K + k + 1)
                    nc.vector.tensor_tensor(xt_lo[:, b, k], ps_x[:, k], xt_hi[:, b, k].bitcast(f32), ALU.subtract).then_inc(xlo_ok, 1)

            def low_h(g, n):
                for k in range(K):
                    dve.wait_ge(hhi_ok[n], g * K + k + 1)
                    nc.vector.tensor_tensor(h_lo[:, n, k], h_full[:, n, k], h_hi[:, n, k].bitcast(f32), ALU.subtract).then_inc(hlo_ok[n], 1)

            def finish(g, b, l3, y_s, stats_s, mv_s, sd_s, rs_s, nb_s):
                for k in range(K):
                    dve.wait_ge(l3, g * K + k + 1)
                    nc.vector.tensor_tensor(y[:, b, 2 * k:2 * k + 2].rearrange("p s d -> p (s d)"), ps_y[:, k],
                                            xb[:, b, 2 * k:2 * k + 2].rearrange("p s d -> p (s d)"), ALU.add).then_inc(y_s, 1)
                dve.wait_ge(y_s, (g + 1) * K)
                for s in range(S):
                    ins = nc.vector.bn_stats(stats[:, s], y[:, b, s])
                ins.then_inc(stats_s, 1)
                dve.wait_ge(w_hi_ok, 1)
                dve.wait_ge(stats_s, g + 1)
                for s in range(S):
                    ins = nc.vector.bn_aggr(mv[:, b, s], stats[:, s])
                ins.then_inc(mv_s, 1)
                dve.wait_ge(sd_s, g + 1)
                nc.vector.reciprocal(rs[:, b], sd[:, b]).then_inc(rs_s, 1)
                dve.wait_ge(rs_s, g + 1)
                nc.vector.scalar_tensor_tensor(nb[:, b], mv[:, b, :, 0], -1.0, rs[:, b], ALU.mult, ALU.mult).then_inc(nb_s, 1)

            def finish_rows(g, b):
                dve.wait_ge(xb_ok, g + 1)
                after(dve, o_ok, g - 1)
                finish(g, b, l3_ps, y_ok, stastage_ok, mv_ok, sd_ok, rs_ok, nb_ok)

            def edges(i, u):
                if u == 0:
                    dve.wait_ge(seg_in, 16 * (i + 1))
                    for k in range(K):
                        dve.wait_ge(xshi_ok, i * K + k + 1)
                        after(dve, run_ok, (i - 1) * K + k + 1)
                        nc.vector.tensor_tensor_scan(run[:, k], seg[:, 0], ps_x[:, k], run[:, k, G - 1:G], ALU.mult, ALU.add)\
                            .then_inc(run_ok, 1)
                    for k in range(K):
                        ins = nc.vector.tensor_tensor(xe_lo[:, 0, k], ps_x[:, k], xe_hi[:, 0, k].bitcast(f32), ALU.subtract)
                    ins.then_inc(xs_ok, 1)
                    dve.wait_ge(run_ok, (i + 1) * K)
                    nc.vector.tensor_tensor(mean[:, :, :], run[:, :, :], seg[:, 1:2].to_broadcast([P, K, G]), ALU.mult).then_inc(mean_ok, 1)
                if u == 1:
                    for k in range(K):
                        dve.wait_ge(xdhi_ok, i * K + k + 1)
                        ins = nc.vector.tensor_tensor(xe_lo[:, 1, k], ps_x[:, k], xe_hi[:, 1, k].bitcast(f32), ALU.subtract)
                    ins.then_inc(xd_ok, 1)
                    dve.wait_ge(mhi_ok, i + 1)
                    nc.vector.tensor_tensor(mean_lo[:, :, :], mean[:, :, :], mean_hi[:, :, :].bitcast(f32), ALU.subtract).then_inc(mlo_ok, 1)

            def body(i, first, last):
                for u in range(U):
                    g = i * U + u
                    if first and u == 0:
                        low_x(g, 0)
                    if not (last and u == U - 1):
                        low_x(g + 1, (u + 1) % 2)
                    low_h(g, 0)
                    if not (first and u == 0):
                        finish_rows(g - 1, (u + 1) % 2)
                    edges(i, u)
                    low_h(g, 1)
                if last:
                    finish_rows(NG - 1, 1)
            passes(dve, body)

            dve.wait_ge(slots_ok, NE)
            nc.vector.tensor_tensor(h_row[:, :], slots[:, :], base[:, :], ALU.min).then_inc(row_ok, 1)
            dve.wait_ge(o_ok, NG)
            nc.vector.memset(run[:, :, :], 0.0).then_inc(c_run_ok, K)

            def front(j, b):
                dve.wait_ge(c_seg_in[b], slot_use(j, b))
                marks, counts = seg_of(b)[:, 0:G], seg_of(b)[:, G:2 * G]
                for k in range(K):
                    dve.wait_ge(c_hs_ok, j * K + k + 1)
                    dve.wait_ge(c_run_ok, j * K + k + 1)
                    nc.vector.tensor_tensor_scan(run[:, k], marks, h_full[:, 0, k], run[:, k, G - 1:G], ALU.mult, ALU.add)\
                        .then_inc(c_run_ok, 1)
                dve.wait_ge(c_run_ok, (j + 2) * K)
                after(dve, c_mhi_ok, j)
                nc.vector.tensor_tensor(mean[:, :, :], run[:, :, :], counts.unsqueeze(1).to_broadcast([P, K, G]), ALU.mult)\
                    .then_inc(c_mean_ok, 1)
                for k in range(K):
                    dve.wait_ge(c_hdhi_ok, j * K + k + 1)
                    nc.vector.tensor_tensor(xe_lo[:, b, k], hd_full[:, k], xe_hi[:, b, k].bitcast(f32), ALU.subtract).then_inc(c_hdlo_ok, 1)

            def mean_low(j, b):
                dve.wait_ge(c_mhi_ok, j + 1)
                nc.vector.tensor_tensor(xt_lo[:, b], mean[:, :, :], xt_hi[:, b].bitcast(f32), ALU.subtract).then_inc(c_mlo_ok, 1)

            def finish_edges(j, b):
                dve.wait_ge(c_xb_in[b], slot_use(j, b))
                after(dve, c_o_ok, j - 1)
                finish(j, b, c_l3_ps, c_y_ok, c_stastage_ok, c_mv_ok, c_sd_ok, c_rs_ok, c_nb_ok)

            front(0, 0)
            mean_low(0, 0)

            def step(j, b, last):
                if not last:
                    front(j + 1, 1 - b)
                for k in range(K):
                    dve.wait_ge(c_hhi_ok, j * K + k + 1)
                    nc.vector.tensor_tensor(h_lo[:, b, k], h_full[:, 1, k], h_hi[:, b, k].bitcast(f32), ALU.subtract).then_inc(c_hlo_ok, 1)
                if not last:
                    mean_low(j + 1, 1 - b)
                if not (isinstance(j, int) and j == 0):
                    finish_edges(j - 1, 1 - b)
                if last:
                    finish_edges(j, b)
            edge_passes(dve, step)

        @block.tensor
        def _(pe):
            pe.wait_ge(cleared, 8)
            pe.wait_ge(prep, PREP_ENDS)
            for n in range(2):
                ins = nc.tensor.transpose(ps_y[:, 0, n * P:(n + 1) * P], tr[:, n], ident[:, :])
            ins.then_inc(turned_pre, 1)
            pe.wait_ge(prep, PREP_CARRY)
            nc.tensor.transpose(ps_y[:, 0, 0:P], tr[:, 2], ident[:, :]).then_inc(turned_pre, 1)
            pe.wait_ge(prep, PREP_IDX)
            for c in range(6):
                ins = nc.tensor.transpose(ps_h1[:, c // S, c % S * P:(c % S + 1) * P], e_idx[:, c // 2, c % 2 * P:(c % 2 + 1) * P], ident[:, :])
            ins.then_inc(turned_pre, 1)
            pe.wait_ge(w_ok, 1)
            pe.wait_ge(idx_ok, 6)

            def turn(ps, rows_of, k):
                for s in range(S):
                    ins = nc.tensor.transpose(ps[:, k, s * P:(s + 1) * P], rows_of[:, s, k * P:(k + 1) * P], ident[:, :])
                return ins

            def columns(parts, ps, m):
                first = True
                for w, hi, lo in parts:
                    for k in range(K):
                        for wx, a in ((w_hi, hi), (w_lo, hi), (w_hi, lo)):
                            end = k == K - 1 and a is lo and w == parts[-1][0]
                            ins = nc.tensor.matmul(ps[:, m], wx[:, w, k, m * P:(m + 1) * P], a[:, k], start=first, stop=end)
                            first = False
                return ins

            def by_rows(parts, ps, s):
                first = True
                for w, hi, lo in parts:
                    for k in range(K):
                        for a, wx in ((hi, w_hi), (hi, w_lo), (lo, w_hi)):
                            end = k == K - 1 and a is lo and w == parts[-1][0]
                            ins = nc.tensor.matmul(ps[:, s // 2, s % 2 * D:(s % 2 + 1) * D], a[:, k, s * P:(s + 1) * P],
                                                   wx[:, w, k], start=first, stop=end)
                            first = False
                return ins

            def turn_rows(i, u, g):
                pe.wait_ge(x_in[u], 16 * (i + 1))
                for k in range(K):
                    turn(ps_x, xn[:, u], k).then_inc(xt_ps, 1)

            def last_layer(g, b, low_ok, y_s, l3):
                pe.wait_ge(low_ok, (g + 1) * K)
                for s in range(S):
                    if s % 2 == 0:
                        after(pe, y_s, (g - 1) * K + s // 2 + 1)
                    ins = by_rows([(X3, h_hi[:, b], h_lo[:, b])], ps_y, s)
                    if s % 2:
                        ins.then_inc(l3, 1)

            def edges(i, u, last):
                xs, xd = (xe_hi[:, 0], xe_lo[:, 0]), (xe_hi[:, 1], xe_lo[:, 1])
                if u == 0:
                    pe.wait_ge(xs_in, 16 * S * (i + 1))
                    for k in range(K):
                        turn(ps_x, xe[:, 0], k).then_inc(xs_ps, 1)
                if u == 1:
                    pe.wait_ge(xd_in, 16 * S * (i + 1))
                    for k in range(K):
                        turn(ps_x, xe[:, 1], k).then_inc(xd_ps, 1)
                if u == 2:
                    pe.wait_ge(xs_ok, i + 1)
                    for s in range(S):
                        ins = by_rows([(X1R, *xs)], ps_x, s)
                        if s % 2:
                            ins.then_inc(src_ps, 1)
                if u == 3:
                    pe.wait_ge(mlo_ok, i + 1)
                    pe.wait_ge(xd_ok, i + 1)
                    for s in range(S):
                        ins = by_rows([(X1R, *xd), (X1L, mean_hi, mean_lo)], ps_x, s)
                        if s % 2:
                            ins.then_inc(dst_ps, 1)

            def ps_x_free(i, u, first):
                if u == 0 and first:
                    pe.wait_ge(xlo_ok, K)
                elif u == 0:
                    pe.wait_ge(dst_ok, i * K)
                elif u == 1:
                    pe.wait_ge(xs_ok, i + 1)
                    pe.wait_ge(run_ok, (i + 1) * K)
                elif u == 2:
                    pe.wait_ge(xd_ok, i + 1)
                else:
                    pe.wait_ge(src_ok, (i + 1) * K)

            def body(i, first, last):
                for u in range(U):
                    g = i * U + u
                    if first and u == 0:
                        turn_rows(i, u, g)
                    ps_x_free(i, u, first)
                    if not (last and u == U - 1):
                        turn_rows(i + (u + 1) // U, (u + 1) % U, g + 1)
                    pe.wait_ge(xlo_ok, (g + 1) * K)
                    after(pe, hf_ok[0], g * K)
                    for m in range(K):
                        columns([(X1R, xt_hi[:, u % 2], xt_lo[:, u % 2])], ps_h1, m).then_inc(l_ps[0], 1)
                    if not (first and u == 0):
                        last_layer(g - 1, 1, hlo_ok[1], y_ok, l3_ps)
                    if not (last and u == U - 1):
                        pe.wait_ge(xlo_ok, (g + 2) * K)
                    edges(i, u, last)
                    pe.wait_ge(hlo_ok[0], (g + 1) * K)
                    after(pe, hf_ok[1], g * K)
                    for m in range(K):
                        columns([(X2R, h_hi[:, 0], h_lo[:, 0])], ps_h2, m).then_inc(l_ps[1], 1)
                if last:
                    last_layer(NG - 1, 1, hlo_ok[1], y_ok, l3_ps)
            passes(pe, body)
            pe.wait_ge(dst_ok, NE * K)
            pe.wait_ge(hf_ok[1], NG * K)
            pe.wait_ge(y_ok, NG * K)

            def turn_edges(j, b):
                pe.wait_ge(c_hs_in[b], slot_use(j, b, 16 * S))
                after(pe, c_hs_ok, j * K)
                for k in range(K):
                    turn(ps_x, xn[:, b], k).then_inc(c_hs_ps, 1)
                pe.wait_ge(c_hd_in[b], slot_use(j, b))
                after(pe, c_hdf_ok, j * K)
                for k in range(K):
                    turn(ps_h1, xn[:, 2 + b], k).then_inc(c_hd_ps, 1)

            turn_edges(0, 0)

            def step(j, b, last):
                if not last:
                    turn_edges(j + 1, 1 - b)
                pe.wait_ge(c_mlo_ok, j + 1)
                pe.wait_ge(c_hdlo_ok, (j + 1) * K)
                after(pe, c_hf_ok, j * K)
                for m in range(K):
                    columns([(X2R, xe_hi[:, b], xe_lo[:, b]), (X2L, xt_hi[:, b], xt_lo[:, b])], ps_h2, m).then_inc(c_l2_ps, 1)
                if not (isinstance(j, int) and j == 0):
                    last_layer(j - 1, 1 - b, c_hlo_ok, c_y_ok, c_l3_ps)
                if last:
                    last_layer(j, b, c_hlo_ok, c_y_ok, c_l3_ps)
            edge_passes(pe, step)


PREP_ENDS = 7
PREP_CARRY = 10
PREP_RDEG = 13
PREP_IDX = 18
PREP_END = 19
_INS = ["x", "src", "dst", "L0_gnn_W1_l", "L0_gnn_b1", "L0_gnn_W1_r", "L0_gnn_W2_l", "L0_gnn_b2",
        "L0_gnn_W2_r", "L0_gnn_W3", "L0_gnn_b3"]
_OUTS = [((100000, 256), "float32")]


def kernel(**inputs):
    import numpy as _np
    import concourse.bacc as _bacc
    from concourse import mybir as _mybir
    from concourse.bass_utils import run_bass_kernel_spmd as _run

    nc = _bacc.Bacc("TRN2", target_bir_lowering=False, num_devices=1)
    arrays, args = {}, []
    for name in _INS:
        a = _np.ascontiguousarray(inputs[name])
        arrays[f"in_{name}_dram"] = a
        args.append(nc.dram_tensor(f"in_{name}_dram", a.shape, _mybir.dt.from_np(a.dtype), kind="ExternalInput").ap())
    for i, (shape, dtype) in enumerate(_OUTS):
        dt = _mybir.dt.from_np(_np.dtype(dtype))
        args.append(nc.dram_tensor(f"out_{i}_dram", shape, dt, kind="ExternalOutput").ap())
    build(nc, *args)
    r = _run(nc, [arrays], core_ids=[0])
    got = tuple(r.results[0][f"out_{i}_dram"] for i in range(len(_OUTS)))
    return got[0]
```

```python
from contextlib import ExitStack

import concourse.bass as bass
from concourse import mybir

P = 128
S = 4
G = S * P
U = 4
EPS = 1e-5
FAR = 1 << 20


def build(nc, x, src, dst, W1_l, b1, W1_r, W2_l, b2, W2_r, W3, b3, out):
    f32, f32r, i32 = mybir.dt.float32, mybir.dt.float32r, mybir.dt.int32
    ALU, ACT = mybir.AluOpType, mybir.ActivationFunctionType
    N, D = x.shape
    E = src.shape[0]
    K = D // P
    NG = -(-N // G)
    NI = NG // U
    NE = -(-E // G)
    EP = NE * G
    NT = EP // P
    Q = EP // 256
    QF, QR = E // 256, E % 256
    assert NG == NI * U and NE == NI and NT == 2 * Q and N < FAR and QF == Q - 1 and D == 256
    HALF = NE
    MIDDLE = HALF // 2
    X1R, X2R, X3, X1L, X2L = range(5)

    with ExitStack() as ctx:
        def sb(name, shape, dt=f32):
            return ctx.enter_context(nc.sbuf_tensor(name, shape, dt))

        def pb(name):
            return ctx.enter_context(nc.psum_tensor(name, [P, K, G], f32))

        def sem(name):
            return ctx.enter_context(nc.semaphore(name))

        h_tab = nc.dram_tensor("h_tab", [2 * EP, D], f32, kind="Internal").ap()
        xdb_tab = nc.dram_tensor("xdb_tab", [EP, D], f32, kind="Internal").ap()
        slot_tab = nc.dram_tensor("slot_tab", [N, 1], i32, kind="Internal").ap()
        seg_tab = nc.dram_tensor("seg_tab", [NE, 2, G], f32, kind="Internal").ap()

        ident = sb("ident", [P, P])
        w_raw = sb("w_raw", [P, 5, K, D])
        w_hi = sb("w_hi", [P, 5, K, D], f32r)
        w_lo = sb("w_lo", [P, 5, K, D], f32r)
        bias = sb("bias", [P, 2, K])
        b3_row = sb("b3_row", [P, D])
        eps = sb("eps", [P, 1])
        xn = sb("xn", [P, U, S, D])
        xb = sb("xb", [P, 2, S, D])
        xt_hi = sb("xt_hi", [P, 2, K, G], f32r)
        xt_lo = sb("xt_lo", [P, 2, K, G], f32r)
        h_full = sb("h_full", [P, 2, K, G])
        h_hi = sb("h_hi", [P, 2, K, G], f32r)
        h_lo = sb("h_lo", [P, 2, K, G], f32r)
        y = sb("y", [P, 2, S, D])
        o = sb("o", [P, 2, S, D])
        stats = sb("stats", [P, S, 6])
        mv = sb("mv", [P, 2, S, 2])
        sd = sb("sd", [P, 2, S])
        rs = sb("rs", [P, 2, S])
        nb = sb("nb", [P, 2, S])
        xe = sb("xe", [P, 2, S, D])
        xe_full = sb("xe_full", [P, K, G])
        xe_hi = sb("xe_hi", [P, 2, K, G], f32r)
        xe_lo = sb("xe_lo", [P, 2, K, G], f32r)
        seg = sb("seg", [P, 2, G])
        run = sb("run", [P, K, G])
        mean = sb("mean", [P, K, G])
        mean_hi = sb("mean_hi", [P, K, G], f32r)
        mean_lo = sb("mean_lo", [P, K, G], f32r)
        src_h = sb("src_h", [P, S, D])
        dst_h = sb("dst_h", [P, S, D])
        xdb = sb("xdb", [P, S, D])
        idx = sb("idx", [P, 3, NT], i32)
        own = sb("own", [P, NT], i32)
        base = sb("base", [P, NT], i32)
        slots = sb("slots", [P, NT], i32)
        h_row = sb("h_row", [P, NT], i32)
        e_stage = sb("e_stage", [P, 2, S], i32)
        t_stage = sb("t_stage", [P, 3, S], i32)
        c_stage = sb("c_stage", [P, 2, 2, S], i32)
        ps_x, ps_h1, ps_h2, ps_y = pb("ps_x"), pb("ps_h1"), pb("ps_h2"), pb("ps_y")
        ps_h = [ps_h1, ps_h2]

        pre = h_full[:, :, :, :].rearrange("p a k g -> p (a k g)")
        e_int = pre[0:Q, 0:1024].bitcast(i32).rearrange("p (a j) -> p a j", a=4)
        fill = pre[:, 1024:1824].bitcast(i32)
        e_f = y[:, :, :, :].rearrange("p a s d -> p (a s) d")[:, 0:4]
        p_src, p_dst, p_prev, p_next = (e_f[0:Q, n] for n in range(4))
        e_w = y[:, :, :, :].rearrange("p a s d -> p (a s) d")
        same, seg_last, count, whole = (e_w[0:Q, n] for n in range(4, 8))
        e_idx = o[:, :, :, :].rearrange("p a s d -> p (a s) d")[:, 0:3]
        tr = o[:, :, :, :].rearrange("p a s d -> p (a s d)")[:, 768:1152].rearrange("p (n c) -> p n c", n=3)
        ones = o[:, :, :, :].rearrange("p a s d -> p (a s d)")[:, 1152:1408]
        rdeg = o[:, :, :, :].rearrange("p a s d -> p (a s d)")[:, 1408:1664]
        rows3 = o[:, :, :, :].rearrange("p a s d -> p (a s d)")[:, 1664:2048].rearrange("p (n c) -> p n c", n=3)

        w_in, b_in, made, cleared, e_in = (sem(n) for n in ("w_in", "b_in", "made", "cleared", "e_in"))
        w_hi_ok, w_ok, prep, turned_pre, idx_ok = (sem(n) for n in ("w_hi_ok", "w_ok", "prep", "turned_pre", "idx_ok"))
        seg_out, fill_out = sem("seg_out"), sem("fill_out")
        x_in = [sem(f"x_in{u}") for u in range(U)]
        y_out = [sem(f"y_out{b}") for b in range(2)]
        xt_ps, xhi_ok, xlo_ok = sem("xt_ps"), sem("xhi_ok"), sem("xlo_ok")
        l_ps = [sem("l1_ps"), sem("l2_ps")]
        l3_ps = sem("l3_ps")
        hf_ok = [sem("h1f_ok"), sem("h2f_ok")]
        hhi_ok = [sem("h1hi_ok"), sem("h2hi_ok")]
        hlo_ok = [sem("h1lo_ok"), sem("h2lo_ok")]
        xb_ok, y_ok, stats_ok, mv_ok, sd_ok, rs_ok, nb_ok, o_ok = (sem(n) for n in (
            "xb_ok", "y_ok", "stats_ok", "mv_ok", "sd_ok", "rs_ok", "nb_ok", "o_ok"))
        xs_in, xd_in, seg_in = sem("xs_in"), sem("xd_in"), sem("seg_in")
        xs_ps, xd_ps, src_ps, dst_ps = sem("xs_ps"), sem("xd_ps"), sem("src_ps"), sem("dst_ps")
        xsf_ok, xdf_ok = sem("xsf_ok"), sem("xdf_ok")
        xshi_ok, xdhi_ok, mhi_ok = sem("xshi_ok"), sem("xdhi_ok"), sem("mhi_ok")
        run_ok, mean_ok, xs_ok, xd_ok, mlo_ok = (sem(n) for n in ("run_ok", "mean_ok", "xs_ok", "xd_ok", "mlo_ok"))
        src_ok, dst_ok, xdb_ok = sem("src_ok"), sem("dst_ok"), sem("xdb_ok")
        src_out, dst_out, xdb_out = sem("src_out"), sem("dst_out"), sem("xdb_out")
        stage_ok, tab_out, slot_in, slots_ok = (sem(n) for n in ("stage_ok", "tab_out", "slot_in", "slots_ok"))
        row_ok = sem("row_ok")
        c_hs_in = [sem(f"c_hs_in{b}") for b in range(2)]
        c_hd_in = [sem(f"c_hd_in{b}") for b in range(2)]
        c_xb_in = [sem(f"c_xb_in{b}") for b in range(2)]
        c_seg_in = [sem(f"c_seg_in{b}") for b in range(2)]
        c_out = [sem(f"c_out{b}") for b in range(2)]
        c_hs_ps, c_hd_ps, c_l2_ps, c_l3_ps = (sem(n) for n in (
            "c_hs_ps", "c_hd_ps", "c_l2_ps", "c_l3_ps"))
        c_hs_ok, c_hdf_ok, c_hdhi_ok, c_hdlo_ok, c_run_ok, c_mean_ok, c_mhi_ok, c_mlo_ok = (sem(n) for n in (
            "c_hs_ok", "c_hdf_ok", "c_hdhi_ok", "c_hdlo_ok", "c_run_ok", "c_mean_ok", "c_mhi_ok", "c_mlo_ok"))
        c_hf_ok, c_hhi_ok, c_hlo_ok, c_y_ok, c_stats_ok, c_mv_ok, c_sd_ok, c_rs_ok, c_nb_ok, c_o_ok = (sem(n) for n in (
            "c_hf_ok", "c_hhi_ok", "c_hlo_ok", "c_y_ok", "c_stats_ok", "c_mv_ok", "c_sd_ok", "c_rs_ok", "c_nb_ok", "c_o_ok"))

        def after(eng, s, value):
            if not (isinstance(value, int) and value <= 0):
                eng.wait_ge(s, value)

        def rows(t, g):
            first = min(g * G, N - G) if isinstance(g, int) else g * G
            return t[bass.ds(first, G), :].rearrange("(p s) d -> p s d", s=S)

        def slots_of(t, j, start=0):
            first = j * G + start
            return t[bass.ds(first, G), :].rearrange("(s p) d -> p s d", p=P)

        def passes(eng, body):
            body(0, True, False)
            with eng.Fori(1, NI - 1) as i:
                body(i, False, False)
            body(NI - 1, False, True)

        def edge_passes(eng, step):
            for j in range(5):
                step(j, j % 2, 2)
            with eng.Fori(0, (NE - 7) // 2) as m:
                step(m * 2 + 5, 1, 2)
                step(m * 2 + 6, 0, 2)
            step(NE - 2, 1, 1)
            step(NE - 1, 0, 0)

        def slot_use(j, parity, n=16):
            return n * ((j - parity) // 2 + 1) if isinstance(j, int) else (j - parity + 2) * (n // 2)

        def seg_of(b):
            return (seg[:, :, :].rearrange("p a g -> p (a g)"), src_h[:, :, :].rearrange("p s d -> p (s d)"))[b]

        hd_full = dst_h[:, :, :].rearrange("p (k a) d -> p k (a d)", k=K)

        block = ctx.enter_context(nc.Block())

        @block.sync
        def _(sp):
            for n, w in enumerate((W1_r, W2_r, W3, W1_l, W2_l)):
                sp.dma_start(w_raw[:, n], w.rearrange("(k p) n -> p k n", p=P)).then_inc(w_in, 16)
            for n, b in enumerate((b1, b2)):
                for k in range(K):
                    sp.dma_start(bias[:, n, k:k + 1], b[k * P:(k + 1) * P].rearrange("(p a) -> p a", a=1)).then_inc(b_in, 16)
            sp.dma_start(b3_row[:, :], b3.rearrange("(a n) -> a n", a=1).to_broadcast([P, D])).then_inc(b_in, 16)
            for u in range(U):
                sp.dma_start(xn[:, u], rows(x, u)).then_inc(x_in[u], 16)
            sp.wait_ge(cleared, 4)
            sp.dma_start(slot_tab.rearrange("(p c) a -> p (c a)", p=125), fill[0:125, :]).then_inc(fill_out, 16)
            sp.wait_ge(prep, PREP_RDEG)
            for h in range(2):
                sp.dma_start(seg_tab[:, 0, h * 256:(h + 1) * 256], same[h:Q:2, :]).then_inc(seg_out, 16)
                sp.dma_start(seg_tab[:, 1, h * 256:(h + 1) * 256], rdeg[h:Q:2, :]).then_inc(seg_out, 16)
            sp.wait_ge(seg_out, 64)

            def store(g, b):
                sp.wait_ge(o_ok, g + 1)
                sp.dma_start(rows(out, g), o[:, b]).then_inc(y_out[b], 16)

            def edge_store(i, u):
                if u == 0:
                    sp.wait_ge(xdb_ok, i + 1)
                    sp.dma_start(slots_of(xdb_tab, i), xdb[:, :, :]).then_inc(xdb_out, 16)
                if u == 2:
                    sp.wait_ge(src_ok, (i + 1) * K)
                    sp.dma_start(slots_of(h_tab, i, EP), src_h[:, :, :]).then_inc(src_out, 16)
                if u == 3:
                    sp.wait_ge(dst_ok, (i + 1) * K)
                    sp.dma_start(slots_of(h_tab, i), dst_h[:, :, :]).then_inc(dst_out, 16)

            def body(i, first, last):
                for u in range(U):
                    g = i * U + u
                    if not first:
                        sp.wait_ge(xt_ps, (g - U + 1) * K)
                        sp.wait_ge(xb_ok, g - U + 1)
                        sp.dma_start(xn[:, u], rows(x, g)).then_inc(x_in[u], 16)
                    if not first:
                        store(g - U, u % 2)
                        edge_store(i - 1, u)
                    if u == 1:
                        after(sp, mean_ok, i)
                        sp.dma_start(seg[:, :, :].rearrange("p a g -> p (a g)"),
                                     seg_tab[bass.ds(i, 1), :, :].rearrange("j a g -> j (a g)").to_broadcast([P, 2 * G]))\
                            .then_inc(seg_in, 16)
            passes(sp, body)
            for g in range(NG - U, NG):
                if g == NG - 1:
                    sp.wait_ge(y_out[(g - 1) % 2], 16 * (NG // 2))
                store(g, g % 2)
                edge_store(NE - 1, g % U)

            sp.wait_ge(dst_out, 16 * NE)
            sp.wait_ge(src_out, 16 * NE)
            sp.wait_ge(xdb_out, 16 * NE)
            sp.wait_ge(mean_ok, NI)
            sp.wait_ge(xb_ok, NG)
            sp.wait_ge(xt_ps, NG * K)
            sp.wait_ge(y_ok, NG * K)

            def load(j, b):
                after(sp, c_hd_ps, (j - 1) * K)
                sp.dma_start(xn[:, 2 + b], slots_of(h_tab, j)).then_inc(c_hd_in[b], 16)
                after(sp, c_mean_ok, j - 1)
                sp.dma_start(seg_of(b), seg_tab[bass.ds(j, 1), :, :].rearrange("j a g -> j (a g)").to_broadcast([P, 2 * G]))\
                    .then_inc(c_seg_in[b], 16)

            def load_x(j, b):
                after(sp, c_y_ok, (j - 1) * K)
                sp.dma_start(xb[:, b], slots_of(xdb_tab, j)).then_inc(c_xb_in[b], 16)

            load(0, 0)
            load(1, 1)
            load_x(0, 0)

            def step(j, b, left):
                if left > 1:
                    load(j + 2, b)
                if left:
                    load_x(j + 1, 1 - b)
            edge_passes(sp, step)

        @block.gpsimd
        def _(pool):
            staged = pool.alloc_register("staged")
            pool.reg_mov(staged, 1)

            def wait_staged():
                pool.wait_ge(stage_ok, pool.snap(staged, min_val=1, max_val=10 * NE))
                pool.reg_add(staged, staged, 1)

            nc.gpsimd.memset(e_int[:, 0], 0).then_inc(made, 1)
            nc.gpsimd.memset(e_int[:, 1:4], N).then_inc(made, 1)
            pool.wait_ge(made, 2)
            nc.gpsimd.memset(e_int[0:1, 2, 0:1], -1).then_inc(cleared, 1)
            nc.gpsimd.memset(fill, FAR).then_inc(cleared, 1)
            nc.gpsimd.memset(e_idx, 0.0).then_inc(cleared, 1)
            nc.gpsimd.memset(tr, 0.0).then_inc(cleared, 1)
            nc.gpsimd.memset(ones, 1.0).then_inc(cleared, 1)
            nc.gpsimd.memset(run[:, :, :], 0.0).then_inc(cleared, 1)
            nc.gpsimd.memset(eps[:, :], EPS).then_inc(cleared, 1)
            nc.gpsimd.memset(ident[:, :], 0.0).then_inc(made, 1)
            pool.wait_ge(made, 3)
            nc.gpsimd.affine_select(out=ident[:, :], in_=ident[:, :], compare_op=ALU.not_equal, fill=1.0,
                                    base=0, pattern=[[-1, P]], channel_multiplier=1).then_inc(cleared, 1)
            nc.gpsimd.iota(own[:, :], [[P, NT]], base=0, channel_multiplier=1).then_inc(cleared, 1)
            nc.gpsimd.iota(base[:, :], [[P, NT]], base=EP, channel_multiplier=1).then_inc(cleared, 1)
            pool.wait_ge(cleared, 10)
            pool.wait_ge(idx_ok, 6)
            pool.wait_ge(fill_out, 16)
            pool.wait_ge(b_in, 80)

            def gather(i, kind, ps, landed):
                after(pool, landed, 16 * S * i)
                after(pool, ps, i * K)
                if kind == 1:
                    after(pool, xdb_ok, i)
                nc.gpsimd.tensor_copy(e_stage[:, kind], idx[:, kind, bass.ds(i * S, S)]).then_inc(stage_ok, 1)
                wait_staged()
                for s in range(S):
                    nc.gpsimd.indirect_dma_start(
                        out=xe[:, kind, s], out_offset=None, in_=x,
                        in_offset=bass.IndirectOffsetOnAxis(ap=e_stage[:, kind, s:s + 1], axis=0)).then_inc(landed, 16)

            def note_slots(n):
                after(pool, tab_out, 16 * S * n)
                nc.gpsimd.tensor_copy(t_stage[:, 0], idx[:, 2, bass.ds(n * S, S)])
                nc.gpsimd.tensor_copy(t_stage[:, 1], own[:, bass.ds(n * S, S)]).then_inc(stage_ok, 1)
                wait_staged()
                for s in range(S):
                    nc.gpsimd.indirect_dma_start(
                        out=slot_tab, out_offset=bass.IndirectOffsetOnAxis(ap=t_stage[:, 0, s:s + 1], axis=0),
                        in_=t_stage[:, 1, s:s + 1], in_offset=None, bounds_check=N - 1, oob_is_err=False).then_inc(tab_out, 16)

            def keep_slots(m):
                pool.wait_ge(slot_in, 16 * S * (m + 1))
                nc.gpsimd.tensor_copy(slots[:, bass.ds(m * S, S)], t_stage[:, 2]).then_inc(slots_ok, 1)

            def look_up(m):
                if isinstance(m, int) and m == 0:
                    pool.wait_ge(tab_out, 16 * S * NE)
                else:
                    keep_slots(m - 1)
                after(pool, slots_ok, m)
                nc.gpsimd.tensor_copy(t_stage[:, 0], idx[:, 0, bass.ds(m * S, S)]).then_inc(stage_ok, 1)
                wait_staged()
                for s in range(S):
                    nc.gpsimd.indirect_dma_start(
                        out=t_stage[:, 2, s:s + 1], out_offset=None, in_=slot_tab,
                        in_offset=bass.IndirectOffsetOnAxis(ap=t_stage[:, 0, s:s + 1], axis=0)).then_inc(slot_in, 16)

            def batch(i, half, phase):
                if phase == 0 or (phase == 1 and half == 0):
                    note_slots(i * 2 + half)
                else:
                    look_up(i * 2 + half - HALF)

            def normalise(b):
                for s in range(S):
                    ins = nc.gpsimd.tensor_scalar(o[:, b, s], y[:, b, s], rs[:, b, s:s + 1], nb[:, b, s:s + 1], ALU.mult, ALU.add)
                ins.then_inc(o_ok, 1)

            def body(i, first, last, phase):
                for u in range(U):
                    g = i * U + u
                    b = u % 2
                    after(pool, nb_ok, g - 1)
                    if not first:
                        pool.wait_ge(y_out[b], 8 * (g - 2 - b))
                    pool.wait_ge(x_in[u], 16 * (i + 1))
                    after(pool, y_ok, (g - 1) * K)
                    nc.gpsimd.tensor_tensor(xb[:, b], xn[:, u],
                                            b3_row[:, :].unsqueeze(1).to_broadcast([P, S, D]), ALU.add).then_inc(xb_ok, 1)
                    if not (first and u < 2):
                        normalise(b)
                    if u == 0:
                        pool.wait_ge(xd_in, 16 * S * (i + 1))
                        after(pool, xdb_out, 16 * i)
                        nc.gpsimd.tensor_tensor(xdb[:, :, :], xe[:, 1],
                                                b3_row[:, :].unsqueeze(1).to_broadcast([P, S, D]), ALU.add).then_inc(xdb_ok, 1)
                        batch(i, 0, phase)
                    if u == 1 and not last:
                        gather(i + 1, 0, xs_ps, xs_in)
                    if u == 2 and not last:
                        gather(i + 1, 1, xd_ps, xd_in)
                    if u == 3:
                        batch(i, 1, phase)

            gather(0, 0, xs_ps, xs_in)
            gather(0, 1, xd_ps, xd_in)
            body(0, True, False, 0)
            with pool.Fori(1, MIDDLE) as i:
                body(i, False, False, 0)
            body(MIDDLE, False, False, 1)
            with pool.Fori(MIDDLE + 1, NI - 1) as i:
                body(i, False, False, 2)
            body(NI - 1, False, True, 2)
            keep_slots(NE - 1)
            for b in range(2):
                pool.wait_ge(nb_ok, NG - 1 + b)
                pool.wait_ge(y_out[b], 16 * (NG // 2 - 1))
                normalise(b)

            pool.wait_ge(row_ok, 1)
            pool.wait_ge(src_out, 16 * NE)
            pool.wait_ge(dst_out, 16 * NE)
            pool.wait_ge(xt_ps, NG * K)
            for b in range(2):
                pool.wait_ge(y_out[b], 16 * (NG // 2))

            def fetch(j, b):
                after(pool, c_hs_in[b], 0 if isinstance(j, int) and j < 2 else slot_use(j - 2, b, 16 * S))
                after(pool, c_hs_ps, (j - 1) * K)
                nc.gpsimd.tensor_copy(c_stage[:, b, 0], h_row[:, bass.ds(j * S, S)]).then_inc(stage_ok, 1)
                wait_staged()
                for s in range(S):
                    nc.gpsimd.indirect_dma_start(
                        out=xn[:, b, s], out_offset=None, in_=h_tab,
                        in_offset=bass.IndirectOffsetOnAxis(ap=c_stage[:, b, 0, s:s + 1], axis=0)).then_inc(c_hs_in[b], 16)

            def scatter(j, b):
                after(pool, c_out[b], 0 if isinstance(j, int) and j < 2 else slot_use(j - 2, b, 16 * S))
                nc.gpsimd.tensor_copy(c_stage[:, b, 1], idx[:, 2, bass.ds(j * S, S)]).then_inc(stage_ok, 1)
                wait_staged()
                pool.wait_ge(c_o_ok, pool.snap(scattered, min_val=1, max_val=NE))
                pool.reg_add(scattered, scattered, 1)
                for s in range(S):
                    nc.gpsimd.indirect_dma_start(
                        out=out, out_offset=bass.IndirectOffsetOnAxis(ap=c_stage[:, b, 1, s:s + 1], axis=0),
                        in_=o[:, b, s], in_offset=None, bounds_check=N - 1, oob_is_err=False).then_inc(c_out[b], 16)

            scattered = pool.alloc_register("scattered")
            pool.reg_mov(scattered, 1)
            fetch(0, 0)
            fetch(1, 1)

            def step(j, b, left):
                if left > 1:
                    fetch(j + 2, b)
                if not (isinstance(j, int) and j < 3):
                    scatter(j - 3, 1 - b)
                if not left:
                    scatter(j - 2, b)
                    scatter(j - 1, 1 - b)
                    scatter(j, b)
            edge_passes(pool, step)
            pool.wait_ge(stage_ok, pool.snap(staged) - 1)
            pool.wait_ge(c_o_ok, pool.snap(scattered) - 1)
            pool.wait_ge(c_out[0], 16 * S * (NE // 2 + 1))
            pool.wait_ge(c_out[1], 16 * S * (NE // 2))

        @block.scalar
        def _(act):
            act.wait_ge(cleared, 1)
            FULL = QF * 256
            act.dma_start(e_int[0:QF, 0], src[0:FULL].rearrange("(q j) -> q j", j=256)).then_inc(e_in, 16)
            act.dma_start(e_int[QF:Q, 0, 0:QR], src[FULL:E].rearrange("(a j) -> a j", a=1)).then_inc(e_in, 16)
            act.dma_start(e_int[0:QF, 1], dst[0:FULL].rearrange("(q j) -> q j", j=256)).then_inc(e_in, 16)
            act.dma_start(e_int[QF:Q, 1, 0:QR], dst[FULL:E].rearrange("(a j) -> a j", a=1)).then_inc(e_in, 16)
            act.dma_start(e_int[0:1, 2, 1:256], dst[0:255].rearrange("(a j) -> a j", a=1)).then_inc(e_in, 16)
            act.dma_start(e_int[1:QF, 2], dst[255:FULL - 1].rearrange("(q j) -> q j", j=256)).then_inc(e_in, 16)
            act.dma_start(e_int[QF:Q, 2, 0:QR + 1], dst[FULL - 1:E].rearrange("(a j) -> a j", a=1)).then_inc(e_in, 16)
            act.dma_start(e_int[0:QF, 3], dst[1:FULL + 1].rearrange("(q j) -> q j", j=256)).then_inc(e_in, 16)
            act.dma_start(e_int[QF:Q, 3, 0:QR - 1], dst[FULL + 1:E].rearrange("(a j) -> a j", a=1)).then_inc(e_in, 16)
            act.wait_ge(w_in, 80)
            nc.scalar.copy(w_hi[:, :, :, :], w_raw[:, :, :, :]).then_inc(w_hi_ok, 1)
            act.wait_ge(b_in, 80)
            act.wait_ge(cleared, 8)
            act.wait_ge(prep, PREP_END)

            def evac_x(g, b):
                for k in range(K):
                    act.wait_ge(xt_ps, g * K + k + 1)
                    nc.scalar.copy(xt_hi[:, b, k], ps_x[:, k]).then_inc(xhi_ok, 1)

            def evac_h(g, n):
                for k in range(K):
                    act.wait_ge(l_ps[n], g * K + k + 1)
                    nc.scalar.activation(h_full[:, n, k], ps_h[n][:, k], ACT.Relu, bias=bias[:, n, k:k + 1]).then_inc(hf_ok[n], 1)
                    act.wait_ge(hf_ok[n], g * K + k + 1)
                    nc.scalar.copy(h_hi[:, n, k], h_full[:, n, k]).then_inc(hhi_ok[n], 1)

            def deviation(g, b):
                act.wait_ge(mv_ok, g + 1)
                nc.scalar.activation(sd[:, b], mv[:, b, :, 1], ACT.Sqrt, bias=eps[:, :]).then_inc(sd_ok, 1)

            def edges(i, u):
                if u == 0:
                    for k in range(K):
                        act.wait_ge(xs_ps, i * K + k + 1)
                        nc.scalar.copy(xe_full[:, k], ps_x[:, k]).then_inc(xsf_ok, 1)
                if u == 1:
                    for k in range(K):
                        act.wait_ge(xd_ps, i * K + k + 1)
                        act.wait_ge(xs_ok, i + 1)
                        act.wait_ge(run_ok, (i + 1) * K)
                        nc.scalar.copy(xe_full[:, k], ps_x[:, k]).then_inc(xdf_ok, 1)
                if u == 2:
                    for k in range(K):
                        act.wait_ge(src_ps, i * K + k + 1)
                        after(act, src_out, 16 * i)
                        nc.scalar.copy(src_h[:, 2 * k:2 * k + 2].rearrange("p s d -> p (s d)"), ps_x[:, k]).then_inc(src_ok, 1)
                if u == 3:
                    for k in range(K):
                        act.wait_ge(dst_ps, i * K + k + 1)
                        after(act, dst_out, 16 * i)
                        nc.scalar.copy(dst_h[:, 2 * k:2 * k + 2].rearrange("p s d -> p (s d)"), ps_x[:, k]).then_inc(dst_ok, 1)

            def edge_parts(i, u):
                if u == 0:
                    act.wait_ge(xsf_ok, (i + 1) * K)
                    nc.scalar.copy(xe_hi[:, 0], xe_full[:, :, :]).then_inc(xshi_ok, 1)
                if u == 1:
                    act.wait_ge(xdf_ok, (i + 1) * K)
                    nc.scalar.copy(xe_hi[:, 1], xe_full[:, :, :]).then_inc(xdhi_ok, 1)
                    act.wait_ge(mean_ok, i + 1)
                    nc.scalar.copy(mean_hi[:, :, :], mean[:, :, :]).then_inc(mhi_ok, 1)

            def body(i, first, last):
                for u in range(U):
                    g = i * U + u
                    if first and u == 0:
                        evac_x(g, 0)
                    evac_h(g, 0)
                    edges(i, u)
                    if not (first and u < 2):
                        deviation(g - 2, u % 2)
                    if not (last and u == U - 1):
                        evac_x(g + 1, (u + 1) % 2)
                    evac_h(g, 1)
                    edge_parts(i, u)
                if last:
                    deviation(NG - 2, 0)
                    deviation(NG - 1, 1)
            passes(act, body)

            def front(j, b):
                for k in range(K):
                    act.wait_ge(c_hs_ps, j * K + k + 1)
                    nc.scalar.activation(h_full[:, 0, k], ps_x[:, k], ACT.Relu, bias=bias[:, 0, k:k + 1]).then_inc(c_hs_ok, 1)
                for k in range(K):
                    act.wait_ge(c_hd_ps, j * K + k + 1)
                    after(act, c_hdlo_ok, j * K)
                    nc.scalar.activation(hd_full[:, k], ps_h1[:, k], ACT.Relu, bias=bias[:, 0, k:k + 1]).then_inc(c_hdf_ok, 1)
                    act.wait_ge(c_hdf_ok, j * K + k + 1)
                    nc.scalar.copy(xe_hi[:, b, k], hd_full[:, k]).then_inc(c_hdhi_ok, 1)

            def mean_high(j, b):
                act.wait_ge(c_mean_ok, j + 1)
                nc.scalar.copy(xt_hi[:, b], mean[:, :, :]).then_inc(c_mhi_ok, 1)

            def second(j, b):
                for k in range(K):
                    after(act, c_hlo_ok, (j - 1) * K + k + 1)
                    act.wait_ge(c_l2_ps, j * K + k + 1)
                    nc.scalar.activation(h_full[:, 1, k], ps_h2[:, k], ACT.Relu, bias=bias[:, 1, k:k + 1]).then_inc(c_hf_ok, 1)
                    act.wait_ge(c_hf_ok, j * K + k + 1)
                    nc.scalar.copy(h_hi[:, b, k], h_full[:, 1, k]).then_inc(c_hhi_ok, 1)

            def tail(j, b):
                act.wait_ge(c_mv_ok, j + 1)
                nc.scalar.activation(sd[:, b], mv[:, b, :, 1], ACT.Sqrt, bias=eps[:, :]).then_inc(c_sd_ok, 1)

            act.wait_ge(dst_out, 16 * NE)
            act.wait_ge(o_ok, NG)
            for b in range(2):
                act.wait_ge(y_out[b], 16 * (NG // 2))
            front(0, 0)
            mean_high(0, 0)

            def step(j, b, left):
                if left:
                    front(j + 1, 1 - b)
                    mean_high(j + 1, 1 - b)
                if not (isinstance(j, int) and j < 2):
                    tail(j - 2, b)
                second(j, b)
                if not left:
                    tail(j - 1, 1 - b)
                    tail(j, b)
            edge_passes(act, step)

        @block.vector
        def _(dve):
            done = [0]

            def link(ins):
                done[0] += 1
                ins.then_inc(prep, 1)
                dve.wait_ge(prep, done[0])

            dve.wait_ge(cleared, 7)
            dve.wait_ge(e_in, 16 * 9)
            link(nc.vector.tensor_copy(e_f[0:Q], e_int))
            link(nc.vector.tensor_tensor(same, p_dst, p_prev, ALU.is_equal))
            link(nc.vector.tensor_tensor(seg_last, p_dst, p_next, ALU.not_equal))
            link(nc.vector.tensor_tensor_scan(count, same, ones[0:Q, :], 0.0, ALU.mult, ALU.add))
            link(nc.vector.tensor_tensor_scan(whole, same, ones[0:Q, :], 1.0, ALU.mult, ALU.mult))
            link(nc.vector.tensor_copy(tr[0:Q, 0, 0:1], count[:, 255:256]))
            link(nc.vector.tensor_copy(tr[0:Q, 1, 0:1], whole[:, 255:256]))
            assert done[0] == PREP_ENDS
            dve.wait_ge(turned_pre, 1)
            link(nc.vector.tensor_copy(rows3[0:1, 0:2], ps_y[0:1, 0, 0:256].rearrange("p (n c) -> p n c", n=2)))
            link(nc.vector.tensor_tensor_scan(rows3[0:1, 2, 0:Q], rows3[0:1, 1, 0:Q], rows3[0:1, 0, 0:Q], 0.0, ALU.mult, ALU.add))
            link(nc.vector.tensor_copy(tr[0:1, 2, 1:Q], rows3[0:1, 2, 0:Q - 1]))
            assert done[0] == PREP_CARRY
            dve.wait_ge(turned_pre, 2)
            link(nc.vector.tensor_copy(rows3[:, 1, 0:1], ps_y[:, 0, 0:1]))
            link(nc.vector.scalar_tensor_tensor(count, whole, rows3[0:Q, 1, 0:1], count, ALU.mult, ALU.add))
            link(nc.vector.reciprocal(rdeg[0:Q, :], count))
            assert done[0] == PREP_RDEG
            link(nc.vector.tensor_copy(e_idx[0:Q, 0], p_src))
            link(nc.vector.tensor_scalar(e_idx[0:Q, 1], p_dst, float(N - 1), None, ALU.min))
            link(nc.vector.tensor_scalar(p_prev, p_dst, float(-FAR), None, ALU.add))
            link(nc.vector.tensor_tensor(p_next, p_prev, seg_last, ALU.mult))
            link(nc.vector.tensor_scalar(e_idx[0:Q, 2], p_next, float(FAR), None, ALU.add))
            assert done[0] == PREP_IDX
            dve.wait_ge(turned_pre, 3)
            for n in range(3):
                for h in range(2):
                    c = (2 * n + h) * P
                    nc.vector.tensor_copy(idx[:, n, h:NT:2], ps_h1[:, c // G, c % G:c % G + Q]).then_inc(idx_ok, 1)
            dve.wait_ge(w_hi_ok, 1)
            nc.vector.tensor_tensor(w_lo[:, :, :, :], w_raw[:, :, :, :], w_hi[:, :, :, :].bitcast(f32), ALU.subtract).then_inc(w_ok, 1)
            dve.wait_ge(seg_out, 64)
            dve.wait_ge(fill_out, 16)
            nc.vector.memset(stats[:, :, :], 0.0).then_inc(prep, 1)
            assert done[0] + 1 == PREP_END

            def low_x(g, b):
                for k in range(K):
                    dve.wait_ge(xhi_ok, g * K + k + 1)
                    nc.vector.tensor_tensor(xt_lo[:, b, k], ps_x[:, k], xt_hi[:, b, k].bitcast(f32), ALU.subtract).then_inc(xlo_ok, 1)

            def low_h(g, n):
                for k in range(K):
                    dve.wait_ge(hhi_ok[n], g * K + k + 1)
                    nc.vector.tensor_tensor(h_lo[:, n, k], h_full[:, n, k], h_hi[:, n, k].bitcast(f32), ALU.subtract).then_inc(hlo_ok[n], 1)

            def residual(g, b, l3, y_s):
                for k in range(K):
                    dve.wait_ge(l3, g * K + k + 1)
                    nc.vector.tensor_tensor(y[:, b, 2 * k:2 * k + 2].rearrange("p s d -> p (s d)"), ps_y[:, k],
                                            xb[:, b, 2 * k:2 * k + 2].rearrange("p s d -> p (s d)"), ALU.add).then_inc(y_s, 1)

            def moments(g, b, y_s, stats_s, mv_s):
                dve.wait_ge(y_s, (g + 1) * K)
                for s in range(S):
                    ins = nc.vector.bn_stats(stats[:, s], y[:, b, s])
                ins.then_inc(stats_s, 1)
                dve.wait_ge(w_hi_ok, 1)
                dve.wait_ge(stats_s, g + 1)
                for s in range(S):
                    ins = nc.vector.bn_aggr(mv[:, b, s], stats[:, s])
                ins.then_inc(mv_s, 1)

            def factors(g, b, sd_s, rs_s, nb_s):
                dve.wait_ge(sd_s, g + 1)
                nc.vector.reciprocal(rs[:, b], sd[:, b]).then_inc(rs_s, 1)
                dve.wait_ge(rs_s, g + 1)
                nc.vector.scalar_tensor_tensor(nb[:, b], mv[:, b, :, 0], -1.0, rs[:, b], ALU.mult, ALU.mult).then_inc(nb_s, 1)

            def residual_rows(g, b):
                dve.wait_ge(xb_ok, g + 1)
                after(dve, o_ok, g - 1)
                residual(g, b, l3_ps, y_ok)

            def moments_rows(g, b):
                moments(g, b, y_ok, stats_ok, mv_ok)

            def factors_rows(g, b):
                factors(g, b, sd_ok, rs_ok, nb_ok)

            def edge_parts(i, u):
                if u == 0:
                    dve.wait_ge(seg_in, 16 * (i + 1))
                    for k in range(K):
                        dve.wait_ge(xsf_ok, i * K + k + 1)
                        after(dve, run_ok, (i - 1) * K + k + 1)
                        nc.vector.tensor_tensor_scan(run[:, k], seg[:, 0], xe_full[:, k], run[:, k, G - 1:G], ALU.mult, ALU.add)\
                            .then_inc(run_ok, 1)
                    dve.wait_ge(xshi_ok, i + 1)
                    nc.vector.tensor_tensor(xe_lo[:, 0], xe_full[:, :, :], xe_hi[:, 0].bitcast(f32), ALU.subtract).then_inc(xs_ok, 1)
                    dve.wait_ge(run_ok, (i + 1) * K)
                    nc.vector.tensor_tensor(mean[:, :, :], run[:, :, :], seg[:, 1:2].to_broadcast([P, K, G]), ALU.mult).then_inc(mean_ok, 1)
                if u == 1:
                    dve.wait_ge(xdhi_ok, i + 1)
                    nc.vector.tensor_tensor(xe_lo[:, 1], xe_full[:, :, :], xe_hi[:, 1].bitcast(f32), ALU.subtract).then_inc(xd_ok, 1)
                    dve.wait_ge(mhi_ok, i + 1)
                    nc.vector.tensor_tensor(mean_lo[:, :, :], mean[:, :, :], mean_hi[:, :, :].bitcast(f32), ALU.subtract).then_inc(mlo_ok, 1)

            def body(i, first, last):
                for u in range(U):
                    g = i * U + u
                    if first and u == 0:
                        low_x(g, 0)
                    low_h(g, 0)
                    if not (first and u < 2):
                        factors_rows(g - 2, u % 2)
                    if not (last and u == U - 1):
                        low_x(g + 1, (u + 1) % 2)
                    if not (first and u == 0):
                        residual_rows(g - 1, (u + 1) % 2)
                    low_h(g, 1)
                    if not (first and u == 0):
                        moments_rows(g - 1, (u + 1) % 2)
                    edge_parts(i, u)
                if last:
                    factors_rows(NG - 2, 0)
                    residual_rows(NG - 1, 1)
                    moments_rows(NG - 1, 1)
                    factors_rows(NG - 1, 1)
            passes(dve, body)

            dve.wait_ge(slots_ok, NE)
            nc.vector.tensor_tensor(h_row[:, :], slots[:, :], base[:, :], ALU.min).then_inc(row_ok, 1)
            dve.wait_ge(o_ok, NG)
            nc.vector.memset(run[:, :, :], 0.0).then_inc(c_run_ok, K)

            def front(j, b):
                dve.wait_ge(c_seg_in[b], slot_use(j, b))
                marks, counts = seg_of(b)[:, 0:G], seg_of(b)[:, G:2 * G]
                for k in range(K):
                    dve.wait_ge(c_hs_ok, j * K + k + 1)
                    dve.wait_ge(c_run_ok, j * K + k + 1)
                    nc.vector.tensor_tensor_scan(run[:, k], marks, h_full[:, 0, k], run[:, k, G - 1:G], ALU.mult, ALU.add)\
                        .then_inc(c_run_ok, 1)
                dve.wait_ge(c_run_ok, (j + 2) * K)
                after(dve, c_mhi_ok, j)
                nc.vector.tensor_tensor(mean[:, :, :], run[:, :, :], counts.unsqueeze(1).to_broadcast([P, K, G]), ALU.mult)\
                    .then_inc(c_mean_ok, 1)
                for k in range(K):
                    dve.wait_ge(c_hdhi_ok, j * K + k + 1)
                    nc.vector.tensor_tensor(xe_lo[:, b, k], hd_full[:, k], xe_hi[:, b, k].bitcast(f32), ALU.subtract).then_inc(c_hdlo_ok, 1)

            def mean_low(j, b):
                dve.wait_ge(c_mhi_ok, j + 1)
                nc.vector.tensor_tensor(xt_lo[:, b], mean[:, :, :], xt_hi[:, b].bitcast(f32), ALU.subtract).then_inc(c_mlo_ok, 1)

            def residual_edges(j, b):
                dve.wait_ge(c_xb_in[b], slot_use(j, b))
                after(dve, c_o_ok, j - 1)
                residual(j, b, c_l3_ps, c_y_ok)
                moments(j, b, c_y_ok, c_stats_ok, c_mv_ok)

            def finish_edges(j, b):
                factors(j, b, c_sd_ok, c_rs_ok, c_nb_ok)
                after(dve, c_out[b], 0 if isinstance(j, int) and j < 2 else slot_use(j - 2, b, 16 * S))
                dve.wait_ge(c_nb_ok, j + 1)
                for s in range(S):
                    ins = nc.vector.tensor_scalar(o[:, b, s], y[:, b, s], rs[:, b, s:s + 1], nb[:, b, s:s + 1], ALU.mult, ALU.add)
                ins.then_inc(c_o_ok, 1)

            front(0, 0)
            mean_low(0, 0)

            def step(j, b, left):
                if left:
                    front(j + 1, 1 - b)
                    mean_low(j + 1, 1 - b)
                if not (isinstance(j, int) and j < 2):
                    finish_edges(j - 2, b)
                for k in range(K):
                    dve.wait_ge(c_hhi_ok, j * K + k + 1)
                    nc.vector.tensor_tensor(h_lo[:, b, k], h_full[:, 1, k], h_hi[:, b, k].bitcast(f32), ALU.subtract).then_inc(c_hlo_ok, 1)
                if not (isinstance(j, int) and j == 0):
                    residual_edges(j - 1, 1 - b)
                if not left:
                    finish_edges(j - 1, 1 - b)
                    residual_edges(j, b)
                    finish_edges(j, b)
            edge_passes(dve, step)

        @block.tensor
        def _(pe):
            pe.wait_ge(cleared, 8)
            pe.wait_ge(prep, PREP_ENDS)
            for n in range(2):
                ins = nc.tensor.transpose(ps_y[:, 0, n * P:(n + 1) * P], tr[:, n], ident[:, :])
            ins.then_inc(turned_pre, 1)
            pe.wait_ge(prep, PREP_CARRY)
            nc.tensor.transpose(ps_y[:, 0, 0:P], tr[:, 2], ident[:, :]).then_inc(turned_pre, 1)
            pe.wait_ge(prep, PREP_IDX)
            for c in range(6):
                ins = nc.tensor.transpose(ps_h1[:, c // S, c % S * P:(c % S + 1) * P], e_idx[:, c // 2, c % 2 * P:(c % 2 + 1) * P], ident[:, :])
            ins.then_inc(turned_pre, 1)
            pe.wait_ge(w_ok, 1)
            pe.wait_ge(idx_ok, 6)

            def turn(ps, rows_of, k):
                for s in range(S):
                    ins = nc.tensor.transpose(ps[:, k, s * P:(s + 1) * P], rows_of[:, s, k * P:(k + 1) * P], ident[:, :])
                return ins

            def columns(parts, ps, m):
                first = True
                for w, hi, lo in parts:
                    for k in range(K):
                        for wx, a in ((w_hi, hi), (w_lo, hi), (w_hi, lo)):
                            end = k == K - 1 and a is lo and w == parts[-1][0]
                            ins = nc.tensor.matmul(ps[:, m], wx[:, w, k, m * P:(m + 1) * P], a[:, k], start=first, stop=end)
                            first = False
                return ins

            def by_rows(parts, ps, s):
                first = True
                for w, hi, lo in parts:
                    for k in range(K):
                        for a, wx in ((hi, w_hi), (hi, w_lo), (lo, w_hi)):
                            end = k == K - 1 and a is lo and w == parts[-1][0]
                            ins = nc.tensor.matmul(ps[:, s // 2, s % 2 * D:(s % 2 + 1) * D], a[:, k, s * P:(s + 1) * P],
                                                   wx[:, w, k], start=first, stop=end)
                            first = False
                return ins

            def turn_rows(i, u, g):
                pe.wait_ge(x_in[u], 16 * (i + 1))
                for k in range(K):
                    turn(ps_x, xn[:, u], k).then_inc(xt_ps, 1)

            def last_layer(g, b, low_ok, y_s, l3):
                pe.wait_ge(low_ok, (g + 1) * K)
                for s in range(S):
                    if s % 2 == 0:
                        after(pe, y_s, (g - 1) * K + s // 2 + 1)
                    ins = by_rows([(X3, h_hi[:, b], h_lo[:, b])], ps_y, s)
                    if s % 2:
                        ins.then_inc(l3, 1)

            def edges(i, u):
                xs, xd = (xe_hi[:, 0], xe_lo[:, 0]), (xe_hi[:, 1], xe_lo[:, 1])
                if u == 0:
                    pe.wait_ge(xs_in, 16 * S * (i + 1))
                    for k in range(K):
                        turn(ps_x, xe[:, 0], k).then_inc(xs_ps, 1)
                if u == 1:
                    pe.wait_ge(xd_in, 16 * S * (i + 1))
                    for k in range(K):
                        turn(ps_x, xe[:, 1], k).then_inc(xd_ps, 1)
                if u == 2:
                    pe.wait_ge(xs_ok, i + 1)
                    for s in range(S):
                        ins = by_rows([(X1R, *xs)], ps_x, s)
                        if s % 2:
                            ins.then_inc(src_ps, 1)
                if u == 3:
                    pe.wait_ge(mlo_ok, i + 1)
                    pe.wait_ge(xd_ok, i + 1)
                    for s in range(S):
                        ins = by_rows([(X1R, *xd), (X1L, mean_hi, mean_lo)], ps_x, s)
                        if s % 2:
                            ins.then_inc(dst_ps, 1)

            def ps_x_free(i, u):
                if u == 0:
                    pe.wait_ge(xsf_ok, (i + 1) * K)
                if u == 1:
                    pe.wait_ge(xdf_ok, (i + 1) * K)
                if u == 2:
                    pe.wait_ge(src_ok, (i + 1) * K)
                if u == 3:
                    pe.wait_ge(dst_ok, (i + 1) * K)

            def body(i, first, last):
                for u in range(U):
                    g = i * U + u
                    if first and u == 0:
                        turn_rows(i, u, g)
                    pe.wait_ge(xlo_ok, (g + 1) * K)
                    after(pe, hf_ok[0], g * K)
                    for m in range(K):
                        columns([(X1R, xt_hi[:, u % 2], xt_lo[:, u % 2])], ps_h1, m).then_inc(l_ps[0], 1)
                    edges(i, u)
                    if not (first and u == 0):
                        last_layer(g - 1, 1, hlo_ok[1], y_ok, l3_ps)
                    if not (last and u == U - 1):
                        ps_x_free(i, u)
                        turn_rows(i + (u + 1) // U, (u + 1) % U, g + 1)
                    pe.wait_ge(hlo_ok[0], (g + 1) * K)
                    after(pe, hf_ok[1], g * K)
                    for m in range(K):
                        columns([(X2R, h_hi[:, 0], h_lo[:, 0])], ps_h2, m).then_inc(l_ps[1], 1)
                if last:
                    last_layer(NG - 1, 1, hlo_ok[1], y_ok, l3_ps)
            passes(pe, body)
            pe.wait_ge(dst_ok, NE * K)
            pe.wait_ge(hf_ok[1], NG * K)
            pe.wait_ge(y_ok, NG * K)

            def turn_edges(j, b):
                pe.wait_ge(c_hs_in[b], slot_use(j, b, 16 * S))
                after(pe, c_hs_ok, j * K)
                for k in range(K):
                    turn(ps_x, xn[:, b], k).then_inc(c_hs_ps, 1)
                pe.wait_ge(c_hd_in[b], slot_use(j, b))
                after(pe, c_hdf_ok, j * K)
                for k in range(K):
                    turn(ps_h1, xn[:, 2 + b], k).then_inc(c_hd_ps, 1)

            turn_edges(0, 0)

            def step(j, b, left):
                if left:
                    turn_edges(j + 1, 1 - b)
                pe.wait_ge(c_mlo_ok, j + 1)
                pe.wait_ge(c_hdlo_ok, (j + 1) * K)
                after(pe, c_hf_ok, j * K)
                for m in range(K):
                    columns([(X2R, xe_hi[:, b], xe_lo[:, b]), (X2L, xt_hi[:, b], xt_lo[:, b])], ps_h2, m).then_inc(c_l2_ps, 1)
                if not (isinstance(j, int) and j == 0):
                    last_layer(j - 1, 1 - b, c_hlo_ok, c_y_ok, c_l3_ps)
                if not left:
                    last_layer(j, b, c_hlo_ok, c_y_ok, c_l3_ps)
            edge_passes(pe, step)


PREP_ENDS = 7
PREP_CARRY = 10
PREP_RDEG = 13
PREP_IDX = 18
PREP_END = 19
_INS = ["x", "src", "dst", "L0_gnn_W1_l", "L0_gnn_b1", "L0_gnn_W1_r", "L0_gnn_W2_l", "L0_gnn_b2",
        "L0_gnn_W2_r", "L0_gnn_W3", "L0_gnn_b3"]
_OUTS = [((100000, 256), "float32")]


def kernel(**inputs):
    import numpy as _np
    import concourse.bacc as _bacc
    from concourse import mybir as _mybir
    from concourse.bass_utils import run_bass_kernel_spmd as _run

    nc = _bacc.Bacc("TRN2", target_bir_lowering=False, num_devices=1)
    arrays, args = {}, []
    for name in _INS:
        a = _np.ascontiguousarray(inputs[name])
        arrays[f"in_{name}_dram"] = a
        args.append(nc.dram_tensor(f"in_{name}_dram", a.shape, _mybir.dt.from_np(a.dtype), kind="ExternalInput").ap())
    for i, (shape, dtype) in enumerate(_OUTS):
        dt = _mybir.dt.from_np(_np.dtype(dtype))
        args.append(nc.dram_tensor(f"out_{i}_dram", shape, dt, kind="ExternalOutput").ap())
    build(nc, *args)
    r = _run(nc, [arrays], core_ids=[0])
    got = tuple(r.results[0][f"out_{i}_dram"] for i in range(len(_OUTS)))
    return got[0]
```

```python
from contextlib import ExitStack

import concourse.bass as bass
from concourse import mybir

P = 128
S = 4
G = S * P
U = 4
EPS = 1e-5
FAR = 1 << 20


def build(nc, x, src, dst, W1_l, b1, W1_r, W2_l, b2, W2_r, W3, b3, out):
    f32, f32r, i32 = mybir.dt.float32, mybir.dt.float32r, mybir.dt.int32
    ALU, ACT = mybir.AluOpType, mybir.ActivationFunctionType
    N, D = x.shape
    E = src.shape[0]
    K = D // P
    NG = -(-N // G)
    NI = NG // U
    NE = -(-E // G)
    EP = NE * G
    NT = EP // P
    Q = EP // 256
    QF, QR = E // 256, E % 256
    assert NG == NI * U and NE == NI and NT == 2 * Q and N < FAR and QF == Q - 1 and D == 256
    HALF = NE
    MIDDLE = HALF // 2
    PEEL = 5
    X1R, X2R, X3, X1L, X2L = range(5)

    with ExitStack() as ctx:
        def sb(name, shape, dt=f32):
            return ctx.enter_context(nc.sbuf_tensor(name, shape, dt))

        def pb(name):
            return ctx.enter_context(nc.psum_tensor(name, [P, K, G], f32))

        def sem(name):
            return ctx.enter_context(nc.semaphore(name))

        h_tab = nc.dram_tensor("h_tab", [2 * EP, D], f32, kind="Internal").ap()
        xdb_tab = nc.dram_tensor("xdb_tab", [EP, D], f32, kind="Internal").ap()
        slot_tab = nc.dram_tensor("slot_tab", [N, 1], i32, kind="Internal").ap()
        seg_tab = nc.dram_tensor("seg_tab", [NE, 2, G], f32, kind="Internal").ap()

        ident = sb("ident", [P, P])
        w_raw = sb("w_raw", [P, 5, K, D])
        w_hi = sb("w_hi", [P, 5, K, D], f32r)
        w_lo = sb("w_lo", [P, 5, K, D], f32r)
        bias = sb("bias", [P, 2, K])
        b1_row = sb("b1_row", [P, D])
        b3_row = sb("b3_row", [P, D])
        eps = sb("eps", [P, 1])
        xn = sb("xn", [P, U, S, D])
        xb = sb("xb", [P, 2, S, D])
        xt_hi = sb("xt_hi", [P, 2, K, G], f32r)
        xt_lo = sb("xt_lo", [P, 2, K, G], f32r)
        h_full = sb("h_full", [P, 2, K, G])
        h_hi = sb("h_hi", [P, 2, K, G], f32r)
        h_lo = sb("h_lo", [P, 2, K, G], f32r)
        y = sb("y", [P, 2, S, D])
        o = sb("o", [P, 2, S, D])
        stats = sb("stats", [P, S, 6])
        mv = sb("mv", [P, 2, S, 2])
        sd = sb("sd", [P, 2, S])
        rs = sb("rs", [P, 2, S])
        nb = sb("nb", [P, 2, S])
        xe = sb("xe", [P, 2, S, D])
        xe_full = sb("xe_full", [P, 2, K, G])
        xe_hi = sb("xe_hi", [P, 2, K, G], f32r)
        xe_lo = sb("xe_lo", [P, 2, K, G], f32r)
        seg = sb("seg", [P, 2, G])
        run = sb("run", [P, K, G])
        mean = sb("mean", [P, K, G])
        mean_hi = sb("mean_hi", [P, K, G], f32r)
        mean_lo = sb("mean_lo", [P, K, G], f32r)
        src_h = sb("src_h", [P, S, D])
        dst_h = sb("dst_h", [P, S, D])
        xdb = sb("xdb", [P, S, D])
        idx = sb("idx", [P, 3, NT], i32)
        own = sb("own", [P, NT], i32)
        base = sb("base", [P, NT], i32)
        slots = sb("slots", [P, NT], i32)
        h_row = sb("h_row", [P, NT], i32)
        e_stage = sb("e_stage", [P, 2, S], i32)
        t_stage = sb("t_stage", [P, 3, S], i32)
        c_stage = sb("c_stage", [P, 2, 2, S], i32)
        ps_x, ps_h1, ps_h2, ps_y = pb("ps_x"), pb("ps_h1"), pb("ps_h2"), pb("ps_y")
        ps_h = [ps_h1, ps_h2]

        pre = h_full[:, :, :, :].rearrange("p a k g -> p (a k g)")
        e_int = pre[0:Q, 0:1024].bitcast(i32).rearrange("p (a j) -> p a j", a=4)
        fill = pre[:, 1024:1824].bitcast(i32)
        e_f = y[:, :, :, :].rearrange("p a s d -> p (a s) d")[:, 0:4]
        p_src, p_dst, p_prev, p_next = (e_f[0:Q, n] for n in range(4))
        e_w = y[:, :, :, :].rearrange("p a s d -> p (a s) d")
        same, seg_last, count, whole = (e_w[0:Q, n] for n in range(4, 8))
        e_idx = o[:, :, :, :].rearrange("p a s d -> p (a s) d")[:, 0:3]
        tr = o[:, :, :, :].rearrange("p a s d -> p (a s d)")[:, 768:1152].rearrange("p (n c) -> p n c", n=3)
        ones = o[:, :, :, :].rearrange("p a s d -> p (a s d)")[:, 1152:1408]
        rdeg = o[:, :, :, :].rearrange("p a s d -> p (a s d)")[:, 1408:1664]
        rows3 = o[:, :, :, :].rearrange("p a s d -> p (a s d)")[:, 1664:2048].rearrange("p (n c) -> p n c", n=3)

        w_in, b_in, made, cleared, e_in = (sem(n) for n in ("w_in", "b_in", "made", "cleared", "e_in"))
        w_hi_ok, w_ok, prep, turned_pre, idx_ok = (sem(n) for n in ("w_hi_ok", "w_ok", "prep", "turned_pre", "idx_ok"))
        seg_out, fill_out = sem("seg_out"), sem("fill_out")
        x_in = [sem(f"x_in{u}") for u in range(U)]
        y_out = [sem(f"y_out{b}") for b in range(2)]
        xt_ps, xhi_ok, xlo_ok = sem("xt_ps"), sem("xhi_ok"), sem("xlo_ok")
        l_ps = [sem("l1_ps"), sem("l2_ps")]
        l3_ps = sem("l3_ps")
        hf_ok = [sem("h1f_ok"), sem("h2f_ok")]
        hhi_ok = [sem("h1hi_ok"), sem("h2hi_ok")]
        hlo_ok = [sem("h1lo_ok"), sem("h2lo_ok")]
        xb_ok, y_ok, stats_ok, mv_ok, sd_ok, rs_ok, nb_ok, o_ok = (sem(n) for n in (
            "xb_ok", "y_ok", "stats_ok", "mv_ok", "sd_ok", "rs_ok", "nb_ok", "o_ok"))
        xs_in, xd_in, seg_in = sem("xs_in"), sem("xd_in"), sem("seg_in")
        xs_ps, xd_ps, src_ps, dst_ps = sem("xs_ps"), sem("xd_ps"), sem("src_ps"), sem("dst_ps")
        xsf_ok, xdf_ok = sem("xsf_ok"), sem("xdf_ok")
        xshi_ok, xdhi_ok, mhi_ok = sem("xshi_ok"), sem("xdhi_ok"), sem("mhi_ok")
        run_ok, mean_ok, xs_ok, xd_ok, mlo_ok = (sem(n) for n in ("run_ok", "mean_ok", "xs_ok", "xd_ok", "mlo_ok"))
        src_ok, dst_ok, xdb_ok = sem("src_ok"), sem("dst_ok"), sem("xdb_ok")
        src_out, dst_out, xdb_out = sem("src_out"), sem("dst_out"), sem("xdb_out")
        stage_ok, tab_out, slot_in, slots_ok = (sem(n) for n in ("stage_ok", "tab_out", "slot_in", "slots_ok"))
        row_ok = sem("row_ok")
        c_hs_in = [sem(f"c_hs_in{b}") for b in range(2)]
        c_hd_in = [sem(f"c_hd_in{b}") for b in range(2)]
        c_xb_in = [sem(f"c_xb_in{b}") for b in range(2)]
        c_seg_in = [sem(f"c_seg_in{b}") for b in range(2)]
        c_out = [sem(f"c_out{b}") for b in range(2)]
        c_hs_ps, c_hd_ps, c_l2_ps, c_l3_ps = (sem(n) for n in (
            "c_hs_ps", "c_hd_ps", "c_l2_ps", "c_l3_ps"))
        c_hs_ok, c_hdhi_ok, c_hdlo_ok, c_run_ok, c_mean_ok, c_mhi_ok, c_mlo_ok = (sem(n) for n in (
            "c_hs_ok", "c_hdhi_ok", "c_hdlo_ok", "c_run_ok", "c_mean_ok", "c_mhi_ok", "c_mlo_ok"))
        c_hf_ok, c_hhi_ok, c_hlo_ok, c_y_ok, c_stats_ok, c_mv_ok, c_sd_ok, c_rs_ok, c_nb_ok, c_o_ok = (sem(n) for n in (
            "c_hf_ok", "c_hhi_ok", "c_hlo_ok", "c_y_ok", "c_stats_ok", "c_mv_ok", "c_sd_ok", "c_rs_ok", "c_nb_ok", "c_o_ok"))

        def after(eng, s, value):
            if not (isinstance(value, int) and value <= 0):
                eng.wait_ge(s, value)

        def rows(t, g):
            first = min(g * G, N - G) if isinstance(g, int) else g * G
            return t[bass.ds(first, G), :].rearrange("(p s) d -> p s d", s=S)

        def slots_of(t, j, start=0):
            first = j * G + start
            return t[bass.ds(first, G), :].rearrange("(s p) d -> p s d", p=P)

        def passes(eng, body):
            body(0, True, False)
            with eng.Fori(1, NI - 1) as i:
                body(i, False, False)
            body(NI - 1, False, True)

        def edge_passes(eng, step):
            for j in range(PEEL):
                step(j, j % 2, 2)
            with eng.Fori(0, (NE - PEEL - 2) // 4) as m:
                for n in range(4):
                    step(m * 4 + (PEEL + n), (PEEL + n) % 2, 2)
            for j in range(PEEL + (NE - PEEL - 2) // 4 * 4, NE):
                step(j, j % 2, min(NE - 1 - j, 2))

        def slot_use(j, parity, n=16):
            return n * ((j - parity) // 2 + 1) if isinstance(j, int) else (j - parity + 2) * (n // 2)

        def seg_of(b):
            return (seg[:, :, :].rearrange("p a g -> p (a g)"), src_h[:, :, :].rearrange("p s d -> p (s d)"))[b]

        block = ctx.enter_context(nc.Block())

        @block.sync
        def _(sp):
            sp.dma_start(xn[:, 0], rows(x, 0)).then_inc(x_in[0], 16)
            for n, w in enumerate((W1_r, W2_r, W3, W1_l, W2_l)):
                if n == 3:
                    sp.wait_ge(cleared, 5)
                sp.dma_start(w_raw[:, n], w.rearrange("(k p) n -> p k n", p=P)).then_inc(w_in, 16)
            sp.wait_ge(e_in, 16 * 9)
            for n, b in enumerate((b1, b2)):
                for k in range(K):
                    sp.dma_start(bias[:, n, k:k + 1], b[k * P:(k + 1) * P].rearrange("(p a) -> p a", a=1)).then_inc(b_in, 16)
            for row, b in ((b1_row, b1), (b3_row, b3)):
                sp.dma_start(row[:, :], b.rearrange("(a n) -> a n", a=1).to_broadcast([P, D])).then_inc(b_in, 16)
            for u in range(1, U):
                sp.dma_start(xn[:, u], rows(x, u)).then_inc(x_in[u], 16)
            sp.wait_ge(cleared, 6)
            sp.dma_start(slot_tab.rearrange("(p c) a -> p (c a)", p=125), fill[0:125, :]).then_inc(fill_out, 16)
            sp.wait_ge(prep, PREP_RDEG)
            for h in range(2):
                sp.dma_start(seg_tab[:, 0, h * 256:(h + 1) * 256], same[h:Q:2, :]).then_inc(seg_out, 16)
                sp.dma_start(seg_tab[:, 1, h * 256:(h + 1) * 256], rdeg[h:Q:2, :]).then_inc(seg_out, 16)
            sp.wait_ge(seg_out, 64)

            def store(g, b):
                sp.wait_ge(o_ok, g + 1)
                sp.dma_start(rows(out, g), o[:, b]).then_inc(y_out[b], 16)

            def edge_store(i, u):
                if u == 0:
                    sp.wait_ge(xdb_ok, i + 1)
                    sp.dma_start(slots_of(xdb_tab, i), xdb[:, :, :]).then_inc(xdb_out, 16)
                if u == 2:
                    sp.wait_ge(src_ok, (i + 1) * K)
                    sp.dma_start(slots_of(h_tab, i, EP), src_h[:, :, :]).then_inc(src_out, 16)
                if u == 3:
                    sp.wait_ge(dst_ok, (i + 1) * K)
                    sp.dma_start(slots_of(h_tab, i), dst_h[:, :, :]).then_inc(dst_out, 16)

            def body(i, first, last):
                for u in range(U):
                    g = i * U + u
                    if not first:
                        sp.wait_ge(xt_ps, (g - U + 1) * K)
                        sp.wait_ge(xb_ok, g - U + 1)
                        sp.dma_start(xn[:, u], rows(x, g)).then_inc(x_in[u], 16)
                    if not first:
                        store(g - U, u % 2)
                        edge_store(i - 1, u)
                    if u == 1:
                        after(sp, mean_ok, i)
                        sp.dma_start(seg[:, :, :].rearrange("p a g -> p (a g)"),
                                     seg_tab[bass.ds(i, 1), :, :].rearrange("j a g -> j (a g)").to_broadcast([P, 2 * G]))\
                            .then_inc(seg_in, 16)
            passes(sp, body)
            store(NG - U, 0)
            edge_store(NE - 1, 0)
            edge_store(NE - 1, 2)
            edge_store(NE - 1, 3)

            sp.wait_ge(dst_out, 16 * NE)
            sp.wait_ge(src_out, 16 * NE)
            sp.wait_ge(xdb_out, 16 * NE)
            sp.wait_ge(mean_ok, NI)
            sp.wait_ge(xb_ok, NG)
            sp.wait_ge(xt_ps, NG * K)

            def load(j, b):
                after(sp, c_hd_ps, (j - 1) * K)
                sp.dma_start(xn[:, 2 + b], slots_of(h_tab, j)).then_inc(c_hd_in[b], 16)
                after(sp, c_mean_ok, j - 1)
                sp.dma_start(seg_of(b), seg_tab[bass.ds(j, 1), :, :].rearrange("j a g -> j (a g)").to_broadcast([P, 2 * G]))\
                    .then_inc(c_seg_in[b], 16)

            def load_x(j, b):
                after(sp, c_y_ok, (j - 1) * K)
                sp.dma_start(xb[:, b], slots_of(xdb_tab, j)).then_inc(c_xb_in[b], 16)

            load(0, 0)
            sp.wait_ge(c_hs_in[0], 16 * S)
            load(1, 1)
            store(NG - 3, 1)
            sp.wait_ge(y_ok, NG * K)
            load_x(0, 0)
            store(NG - 2, 0)
            sp.wait_ge(y_out[0], 16 * (NG // 2))
            store(NG - 1, 1)

            def step(j, b, left):
                if left > 1:
                    load(j + 2, b)
                if left:
                    load_x(j + 1, 1 - b)
            edge_passes(sp, step)

        @block.gpsimd
        def _(pool):
            staged = pool.alloc_register("staged")
            pool.reg_mov(staged, 1)

            def wait_staged():
                pool.wait_ge(stage_ok, pool.snap(staged, min_val=1, max_val=10 * NE))
                pool.reg_add(staged, staged, 1)

            nc.gpsimd.memset(e_int[:, 0], 0).then_inc(made, 1)
            nc.gpsimd.memset(e_int[:, 1:4], N).then_inc(made, 1)
            pool.wait_ge(made, 2)
            nc.gpsimd.memset(e_int[0:1, 2, 0:1], -1).then_inc(cleared, 1)
            nc.gpsimd.memset(ident[:, :], 0.0).then_inc(made, 1)
            pool.wait_ge(made, 3)
            nc.gpsimd.affine_select(out=ident[:, :], in_=ident[:, :], compare_op=ALU.not_equal, fill=1.0,
                                    base=0, pattern=[[-1, P]], channel_multiplier=1).then_inc(cleared, 1)
            nc.gpsimd.memset(tr, 0.0).then_inc(cleared, 1)
            nc.gpsimd.memset(e_idx, 0.0).then_inc(cleared, 1)
            nc.gpsimd.memset(ones, 1.0).then_inc(cleared, 1)
            nc.gpsimd.memset(fill, FAR).then_inc(cleared, 1)
            nc.gpsimd.memset(run[:, :, :], 0.0).then_inc(cleared, 1)
            nc.gpsimd.memset(eps[:, :], EPS).then_inc(cleared, 1)
            nc.gpsimd.iota(own[:, :], [[P, NT]], base=0, channel_multiplier=1).then_inc(cleared, 1)
            nc.gpsimd.iota(base[:, :], [[P, NT]], base=EP, channel_multiplier=1).then_inc(cleared, 1)
            pool.wait_ge(cleared, 10)
            pool.wait_ge(idx_ok, 6)

            def gather(i, kind, ps, landed):
                after(pool, landed, 16 * S * i)
                after(pool, ps, i * K)
                if kind == 1:
                    after(pool, xdb_ok, i)
                nc.gpsimd.tensor_copy(e_stage[:, kind], idx[:, kind, bass.ds(i * S, S)]).then_inc(stage_ok, 1)
                wait_staged()
                for s in range(S):
                    nc.gpsimd.indirect_dma_start(
                        out=xe[:, kind, s], out_offset=None, in_=x,
                        in_offset=bass.IndirectOffsetOnAxis(ap=e_stage[:, kind, s:s + 1], axis=0)).then_inc(landed, 16)

            def note_slots(n):
                after(pool, tab_out, 16 * S * n)
                nc.gpsimd.tensor_copy(t_stage[:, 0], idx[:, 2, bass.ds(n * S, S)])
                nc.gpsimd.tensor_copy(t_stage[:, 1], own[:, bass.ds(n * S, S)]).then_inc(stage_ok, 1)
                wait_staged()
                for s in range(S):
                    nc.gpsimd.indirect_dma_start(
                        out=slot_tab, out_offset=bass.IndirectOffsetOnAxis(ap=t_stage[:, 0, s:s + 1], axis=0),
                        in_=t_stage[:, 1, s:s + 1], in_offset=None, bounds_check=N - 1, oob_is_err=False).then_inc(tab_out, 16)

            def keep_slots(m):
                pool.wait_ge(slot_in, 16 * S * (m + 1))
                nc.gpsimd.tensor_copy(slots[:, bass.ds(m * S, S)], t_stage[:, 2]).then_inc(slots_ok, 1)

            def look_up(m):
                if isinstance(m, int) and m == 0:
                    pool.wait_ge(tab_out, 16 * S * NE)
                else:
                    keep_slots(m - 1)
                after(pool, slots_ok, m)
                nc.gpsimd.tensor_copy(t_stage[:, 0], idx[:, 0, bass.ds(m * S, S)]).then_inc(stage_ok, 1)
                wait_staged()
                for s in range(S):
                    nc.gpsimd.indirect_dma_start(
                        out=t_stage[:, 2, s:s + 1], out_offset=None, in_=slot_tab,
                        in_offset=bass.IndirectOffsetOnAxis(ap=t_stage[:, 0, s:s + 1], axis=0)).then_inc(slot_in, 16)

            def batch(i, half, phase):
                if phase == 0 or (phase == 1 and half == 0):
                    note_slots(i * 2 + half)
                else:
                    look_up(i * 2 + half - HALF)

            def normalise(b):
                for s in range(S):
                    ins = nc.gpsimd.tensor_scalar(o[:, b, s], y[:, b, s], rs[:, b, s:s + 1], nb[:, b, s:s + 1], ALU.mult, ALU.add)
                ins.then_inc(o_ok, 1)

            def body(i, first, last, phase):
                for u in range(U):
                    g = i * U + u
                    b = u % 2
                    after(pool, nb_ok, g - 1)
                    if not first:
                        pool.wait_ge(y_out[b], 8 * (g - 2 - b))
                    pool.wait_ge(x_in[u], 16 * (i + 1))
                    after(pool, y_ok, (g - 1) * K)
                    nc.gpsimd.tensor_tensor(xb[:, b], xn[:, u],
                                            b3_row[:, :].unsqueeze(1).to_broadcast([P, S, D]), ALU.add).then_inc(xb_ok, 1)
                    if not (first and u < 2):
                        normalise(b)
                    if last and u == 2:
                        keep_slots(NE - 1)
                    if u == 0:
                        pool.wait_ge(xd_in, 16 * S * (i + 1))
                        after(pool, xdb_out, 16 * i)
                        nc.gpsimd.tensor_tensor(xdb[:, :, :], xe[:, 1],
                                                b3_row[:, :].unsqueeze(1).to_broadcast([P, S, D]), ALU.add).then_inc(xdb_ok, 1)
                        batch(i, 0, phase)
                    if u == 1 and not last:
                        gather(i + 1, 0, xs_ps, xs_in)
                    if u == 2 and not last:
                        gather(i + 1, 1, xd_ps, xd_in)
                    if u == (1 if last else 3):
                        batch(i, 1, phase)

            gather(0, 0, xs_ps, xs_in)
            gather(0, 1, xd_ps, xd_in)
            pool.wait_ge(fill_out, 16)
            pool.wait_ge(b_in, 96)
            body(0, True, False, 0)
            with pool.Fori(1, MIDDLE) as i:
                body(i, False, False, 0)
            body(MIDDLE, False, False, 1)
            with pool.Fori(MIDDLE + 1, NI - 1) as i:
                body(i, False, False, 2)
            body(NI - 1, False, True, 2)

            def normalise_last(g, b):
                pool.wait_ge(nb_ok, g + 1)
                pool.wait_ge(y_out[b], 16 * (NG // 2 - 1))
                normalise(b)

            pool.wait_ge(row_ok, 1)
            pool.wait_ge(src_out, 16 * NE)
            pool.wait_ge(dst_out, 16 * NE)
            pool.wait_ge(xt_ps, NG * K)

            def fetch(j, b):
                after(pool, c_hs_in[b], 0 if isinstance(j, int) and j < 2 else slot_use(j - 2, b, 16 * S))
                after(pool, c_hs_ps, (j - 1) * K)
                nc.gpsimd.tensor_copy(c_stage[:, b, 0], h_row[:, bass.ds(j * S, S)]).then_inc(stage_ok, 1)
                wait_staged()
                for s in range(S):
                    nc.gpsimd.indirect_dma_start(
                        out=xn[:, b, s], out_offset=None, in_=h_tab,
                        in_offset=bass.IndirectOffsetOnAxis(ap=c_stage[:, b, 0, s:s + 1], axis=0)).then_inc(c_hs_in[b], 16)

            def scatter(j, b):
                after(pool, c_out[b], 0 if isinstance(j, int) and j < 2 else slot_use(j - 2, b, 16 * S))
                nc.gpsimd.tensor_copy(c_stage[:, b, 1], idx[:, 2, bass.ds(j * S, S)]).then_inc(stage_ok, 1)
                wait_staged()
                pool.wait_ge(c_o_ok, pool.snap(scattered, min_val=1, max_val=NE))
                pool.reg_add(scattered, scattered, 1)
                for s in range(S):
                    nc.gpsimd.indirect_dma_start(
                        out=out, out_offset=bass.IndirectOffsetOnAxis(ap=c_stage[:, b, 1, s:s + 1], axis=0),
                        in_=o[:, b, s], in_offset=None, bounds_check=N - 1, oob_is_err=False).then_inc(c_out[b], 16)

            scattered = pool.alloc_register("scattered")
            pool.reg_mov(scattered, 1)
            fetch(0, 0)
            normalise_last(NG - 2, 0)
            fetch(1, 1)
            normalise_last(NG - 1, 1)
            for b in range(2):
                pool.wait_ge(y_out[b], 16 * (NG // 2))

            def step(j, b, left):
                if left > 1:
                    fetch(j + 2, b)
                if not (isinstance(j, int) and j < 3):
                    scatter(j - 3, 1 - b)
                if not left:
                    scatter(j - 2, b)
                    scatter(j - 1, 1 - b)
                    scatter(j, b)
            edge_passes(pool, step)
            pool.wait_ge(stage_ok, pool.snap(staged) - 1)
            pool.wait_ge(c_o_ok, pool.snap(scattered) - 1)
            pool.wait_ge(c_out[0], 16 * S * (NE // 2 + 1))
            pool.wait_ge(c_out[1], 16 * S * (NE // 2))

        @block.scalar
        def _(act):
            act.wait_ge(cleared, 1)
            FULL = QF * 256
            act.dma_start(e_int[0:QF, 0], src[0:FULL].rearrange("(q j) -> q j", j=256)).then_inc(e_in, 16)
            act.dma_start(e_int[QF:Q, 0, 0:QR], src[FULL:E].rearrange("(a j) -> a j", a=1)).then_inc(e_in, 16)
            act.dma_start(e_int[0:QF, 1], dst[0:FULL].rearrange("(q j) -> q j", j=256)).then_inc(e_in, 16)
            act.dma_start(e_int[QF:Q, 1, 0:QR], dst[FULL:E].rearrange("(a j) -> a j", a=1)).then_inc(e_in, 16)
            act.dma_start(e_int[0:1, 2, 1:256], dst[0:255].rearrange("(a j) -> a j", a=1)).then_inc(e_in, 16)
            act.dma_start(e_int[1:QF, 2], dst[255:FULL - 1].rearrange("(q j) -> q j", j=256)).then_inc(e_in, 16)
            act.dma_start(e_int[QF:Q, 2, 0:QR + 1], dst[FULL - 1:E].rearrange("(a j) -> a j", a=1)).then_inc(e_in, 16)
            act.dma_start(e_int[0:QF, 3], dst[1:FULL + 1].rearrange("(q j) -> q j", j=256)).then_inc(e_in, 16)
            act.dma_start(e_int[QF:Q, 3, 0:QR - 1], dst[FULL + 1:E].rearrange("(a j) -> a j", a=1)).then_inc(e_in, 16)
            act.wait_ge(w_in, 80)
            nc.scalar.copy(w_hi[:, :, :, :], w_raw[:, :, :, :]).then_inc(w_hi_ok, 1)
            def evac_x(g, b):
                for k in range(K):
                    act.wait_ge(xt_ps, g * K + k + 1)
                    nc.scalar.copy(xt_hi[:, b, k], ps_x[:, k]).then_inc(xhi_ok, 1)

            def evac_h(g, n):
                for k in range(K):
                    act.wait_ge(l_ps[n], g * K + k + 1)
                    nc.scalar.activation(h_full[:, n, k], ps_h[n][:, k], ACT.Relu, bias=bias[:, n, k:k + 1]).then_inc(hf_ok[n], 1)
                    act.wait_ge(hf_ok[n], g * K + k + 1)
                    nc.scalar.copy(h_hi[:, n, k], h_full[:, n, k]).then_inc(hhi_ok[n], 1)

            def deviation(g, b):
                act.wait_ge(mv_ok, g + 1)
                nc.scalar.activation(sd[:, b], mv[:, b, :, 1], ACT.Sqrt, bias=eps[:, :]).then_inc(sd_ok, 1)

            def edges(i, u):
                if u == 0:
                    for k in range(K):
                        act.wait_ge(xs_ps, i * K + k + 1)
                        after(act, run_ok, i * K)
                        after(act, xs_ok, i)
                        nc.scalar.copy(xe_full[:, 0, k], ps_x[:, k]).then_inc(xsf_ok, 1)
                if u == 1:
                    for k in range(K):
                        act.wait_ge(xd_ps, i * K + k + 1)
                        after(act, xd_ok, i)
                        nc.scalar.copy(xe_full[:, 1, k], ps_x[:, k]).then_inc(xdf_ok, 1)
                if u == 2:
                    act.wait_ge(mean_ok, i + 1)
                    nc.scalar.copy(mean_hi[:, :, :], mean[:, :, :]).then_inc(mhi_ok, 1)

            def edge_parts(i, u):
                if u == 0:
                    act.wait_ge(xsf_ok, (i + 1) * K)
                    nc.scalar.copy(xe_hi[:, 0], xe_full[:, 0]).then_inc(xshi_ok, 1)
                if u == 1:
                    act.wait_ge(xdf_ok, (i + 1) * K)
                    nc.scalar.copy(xe_hi[:, 1], xe_full[:, 1]).then_inc(xdhi_ok, 1)

            evac_x(0, 0)
            act.wait_ge(b_in, 96)
            act.wait_ge(cleared, 8)
            act.wait_ge(prep, PREP_IDX)
            act.wait_ge(fill_out, 16)

            def body(i, first, last):
                for u in range(U):
                    g = i * U + u
                    evac_h(g, 0)
                    edges(i, u)
                    if not (first and u < 2):
                        deviation(g - 2, u % 2)
                    if not (last and u == U - 1):
                        evac_x(g + 1, (u + 1) % 2)
                    evac_h(g, 1)
                    edge_parts(i, u)
                if last:
                    deviation(NG - 2, 0)
                    deviation(NG - 1, 1)
            passes(act, body)

            def front(j, b):
                for k in range(K):
                    act.wait_ge(c_hs_ps, j * K + k + 1)
                    nc.scalar.activation(h_full[:, 0, k], ps_x[:, k], ACT.Relu).then_inc(c_hs_ok, 1)
                for k in range(K):
                    act.wait_ge(c_hd_ps, j * K + k + 1)
                    nc.scalar.activation(xe_hi[:, b, k], ps_h1[:, k], ACT.Relu).then_inc(c_hdhi_ok, 1)

            def mean_high(j, b):
                act.wait_ge(c_mean_ok, j + 1)
                nc.scalar.copy(xt_hi[:, b], mean[:, :, :]).then_inc(c_mhi_ok, 1)

            def second(j, b, k):
                after(act, c_hlo_ok, (j - 1) * K + k + 1)
                act.wait_ge(c_l2_ps, j * K + k + 1)
                nc.scalar.activation(h_full[:, 1, k], ps_h2[:, k], ACT.Relu, bias=bias[:, 1, k:k + 1]).then_inc(c_hf_ok, 1)
                act.wait_ge(c_hf_ok, j * K + k + 1)
                nc.scalar.copy(h_hi[:, b, k], h_full[:, 1, k]).then_inc(c_hhi_ok, 1)

            def deviation_edges(j, b):
                act.wait_ge(c_mv_ok, j + 1)
                nc.scalar.activation(sd[:, b], mv[:, b, :, 1], ACT.Sqrt, bias=eps[:, :]).then_inc(c_sd_ok, 1)

            def finish_edges(j, b):
                after(act, c_out[b], 0 if isinstance(j, int) and j < 2 else slot_use(j - 2, b, 16 * S))
                act.wait_ge(c_nb_ok, j + 1)
                for s in range(S):
                    ins = nc.scalar.activation(o[:, b, s], y[:, b, s], ACT.Identity, bias=nb[:, b, s:s + 1], scale=rs[:, b, s:s + 1])
                ins.then_inc(c_o_ok, 1)

            act.wait_ge(dst_out, 16 * NE)
            act.wait_ge(hlo_ok[1], NG * K)
            front(0, 0)
            mean_high(0, 0)

            def step(j, b, left):
                if left:
                    front(j + 1, 1 - b)
                if not (isinstance(j, int) and j < 2):
                    deviation_edges(j - 2, b)
                second(j, b, 0)
                if left:
                    mean_high(j + 1, 1 - b)
                second(j, b, 1)
                if isinstance(j, int) and j == 0:
                    act.wait_ge(o_ok, NG)
                    for n in range(2):
                        act.wait_ge(y_out[n], 16 * (NG // 2))
                if not (isinstance(j, int) and j < 2):
                    finish_edges(j - 2, b)
                if not left:
                    for n, c in ((j - 1, 1 - b), (j, b)):
                        deviation_edges(n, c)
                        finish_edges(n, c)
            edge_passes(act, step)

        @block.vector
        def _(dve):
            done = [0]

            def link(ins):
                done[0] += 1
                ins.then_inc(prep, 1)
                dve.wait_ge(prep, done[0])

            dve.wait_ge(cleared, 5)
            dve.wait_ge(e_in, 16 * 9)
            link(nc.vector.tensor_copy(e_f[0:Q], e_int))
            link(nc.vector.tensor_tensor(seg_last, p_dst, p_next, ALU.not_equal))
            link(nc.vector.tensor_tensor(same, p_dst, p_prev, ALU.is_equal))
            link(nc.vector.tensor_copy(e_idx[0:Q, 0], p_src))
            link(nc.vector.tensor_scalar(e_idx[0:Q, 1], p_dst, float(N - 1), None, ALU.min))
            link(nc.vector.tensor_scalar(p_prev, p_dst, float(-FAR), None, ALU.add))
            link(nc.vector.tensor_tensor(p_next, p_prev, seg_last, ALU.mult))
            link(nc.vector.tensor_scalar(e_idx[0:Q, 2], p_next, float(FAR), None, ALU.add))
            assert done[0] == PREP_IDX
            link(nc.vector.tensor_tensor_scan(count, same, ones[0:Q, :], 0.0, ALU.mult, ALU.add))
            link(nc.vector.tensor_tensor_scan(whole, same, ones[0:Q, :], 1.0, ALU.mult, ALU.mult))
            link(nc.vector.tensor_copy(tr[0:Q, 0, 0:1], count[:, 255:256]))
            link(nc.vector.tensor_copy(tr[0:Q, 1, 0:1], whole[:, 255:256]))
            assert done[0] == PREP_ENDS
            dve.wait_ge(turned_pre, 1)
            for n in range(3):
                for h in range(2):
                    c = (2 * n + h) * P
                    nc.vector.tensor_copy(idx[:, n, h:NT:2], ps_h2[:, c // G, c % G:c % G + Q]).then_inc(idx_ok, 1)
            dve.wait_ge(turned_pre, 2)
            link(nc.vector.tensor_copy(rows3[0:1, 0:2], ps_y[0:1, 0, 0:256].rearrange("p (n c) -> p n c", n=2)))
            link(nc.vector.tensor_tensor_scan(rows3[0:1, 2, 0:Q], rows3[0:1, 1, 0:Q], rows3[0:1, 0, 0:Q], 0.0, ALU.mult, ALU.add))
            link(nc.vector.tensor_copy(tr[0:1, 2, 1:Q], rows3[0:1, 2, 0:Q - 1]))
            assert done[0] == PREP_CARRY
            dve.wait_ge(w_hi_ok, 1)
            nc.vector.tensor_tensor(w_lo[:, X1R], w_raw[:, X1R], w_hi[:, X1R].bitcast(f32), ALU.subtract).then_inc(w_ok, 1)

            def low_x(g, b):
                for k in range(K):
                    dve.wait_ge(xhi_ok, g * K + k + 1)
                    nc.vector.tensor_tensor(xt_lo[:, b, k], ps_x[:, k], xt_hi[:, b, k].bitcast(f32), ALU.subtract).then_inc(xlo_ok, 1)

            low_x(0, 0)
            nc.vector.tensor_tensor(w_lo[:, X1R + 1:], w_raw[:, X1R + 1:], w_hi[:, X1R + 1:].bitcast(f32), ALU.subtract).then_inc(w_ok, 1)
            dve.wait_ge(turned_pre, 3)
            link(nc.vector.tensor_copy(rows3[:, 1, 0:1], ps_y[:, 0, 0:1]))
            link(nc.vector.scalar_tensor_tensor(count, whole, rows3[0:Q, 1, 0:1], count, ALU.mult, ALU.add))
            link(nc.vector.reciprocal(rdeg[0:Q, :], count))
            assert done[0] == PREP_RDEG
            dve.wait_ge(cleared, 7)

            def low_h(g, n):
                for k in range(K):
                    dve.wait_ge(hhi_ok[n], g * K + k + 1)
                    nc.vector.tensor_tensor(h_lo[:, n, k], h_full[:, n, k], h_hi[:, n, k].bitcast(f32), ALU.subtract).then_inc(hlo_ok[n], 1)

            def residual(g, b, l3, y_s):
                for k in range(K):
                    dve.wait_ge(l3, g * K + k + 1)
                    nc.vector.tensor_tensor(y[:, b, 2 * k:2 * k + 2].rearrange("p s d -> p (s d)"), ps_y[:, k],
                                            xb[:, b, 2 * k:2 * k + 2].rearrange("p s d -> p (s d)"), ALU.add).then_inc(y_s, 1)

            def moments(g, b, y_s, stats_s, mv_s):
                sums(g, b, y_s, stats_s)
                averages(g, b, stats_s, mv_s)

            def sums(g, b, y_s, stats_s):
                dve.wait_ge(y_s, (g + 1) * K)
                for s in range(S):
                    ins = nc.vector.bn_stats(stats[:, s], y[:, b, s])
                ins.then_inc(stats_s, 1)

            def averages(g, b, stats_s, mv_s):
                dve.wait_ge(w_hi_ok, 1)
                dve.wait_ge(stats_s, g + 1)
                aggregate(b, mv_s)

            def aggregate(b, mv_s):
                for s in range(S):
                    ins = nc.vector.bn_aggr(mv[:, b, s], stats[:, s])
                ins.then_inc(mv_s, 1)

            def factors(g, b, sd_s, rs_s, nb_s):
                dve.wait_ge(sd_s, g + 1)
                nc.vector.reciprocal(rs[:, b], sd[:, b]).then_inc(rs_s, 1)
                dve.wait_ge(rs_s, g + 1)
                nc.vector.scalar_tensor_tensor(nb[:, b], mv[:, b, :, 0], -1.0, rs[:, b], ALU.mult, ALU.mult).then_inc(nb_s, 1)

            def residual_rows(g, b):
                dve.wait_ge(xb_ok, g + 1)
                after(dve, o_ok, g - 1)
                residual(g, b, l3_ps, y_ok)

            def moments_rows(g, b):
                moments(g, b, y_ok, stats_ok, mv_ok)

            def factors_rows(g, b):
                factors(g, b, sd_ok, rs_ok, nb_ok)

            def edges(i, u):
                if u == 2:
                    after(dve, src_out, 16 * i)
                    for k in range(K):
                        dve.wait_ge(src_ps, i * K + k + 1)
                        nc.vector.tensor_tensor(src_h[:, 2 * k:2 * k + 2], ps_x[:, k].rearrange("p (s d) -> p s d", s=2),
                                                b1_row[:, :].unsqueeze(1).to_broadcast([P, 2, D]), ALU.add).then_inc(src_ok, 1)
                if u == 3:
                    after(dve, dst_out, 16 * i)
                    for k in range(K):
                        dve.wait_ge(dst_ps, i * K + k + 1)
                        nc.vector.tensor_tensor(dst_h[:, 2 * k:2 * k + 2], ps_x[:, k].rearrange("p (s d) -> p s d", s=2),
                                                b1_row[:, :].unsqueeze(1).to_broadcast([P, 2, D]), ALU.add).then_inc(dst_ok, 1)

            def edge_parts(i, u):
                if u == 0:
                    dve.wait_ge(seg_in, 16 * (i + 1))
                    for k in range(K):
                        dve.wait_ge(xsf_ok, i * K + k + 1)
                        after(dve, run_ok, (i - 1) * K + k + 1)
                        nc.vector.tensor_tensor_scan(run[:, k], seg[:, 0], xe_full[:, 0, k], run[:, k, G - 1:G], ALU.mult, ALU.add)\
                            .then_inc(run_ok, 1)
                if u == 1:
                    dve.wait_ge(xshi_ok, i + 1)
                    nc.vector.tensor_tensor(xe_lo[:, 0], xe_full[:, 0], xe_hi[:, 0].bitcast(f32), ALU.subtract).then_inc(xs_ok, 1)
                    dve.wait_ge(run_ok, (i + 1) * K)
                    nc.vector.tensor_tensor(mean[:, :, :], run[:, :, :], seg[:, 1:2].to_broadcast([P, K, G]), ALU.mult).then_inc(mean_ok, 1)
                if u == 2:
                    dve.wait_ge(xdhi_ok, i + 1)
                    nc.vector.tensor_tensor(xe_lo[:, 1], xe_full[:, 1], xe_hi[:, 1].bitcast(f32), ALU.subtract).then_inc(xd_ok, 1)
                    dve.wait_ge(mhi_ok, i + 1)
                    nc.vector.tensor_tensor(mean_lo[:, :, :], mean[:, :, :], mean_hi[:, :, :].bitcast(f32), ALU.subtract).then_inc(mlo_ok, 1)

            def body(i, first, last):
                for u in range(U):
                    g = i * U + u
                    if u == 2:
                        edges(i, u)
                    low_h(g, 0)
                    if not (first and u < 2):
                        factors_rows(g - 2, u % 2)
                    if u == 3:
                        edges(i, u)
                    if not (last and u == U - 1):
                        low_x(g + 1, (u + 1) % 2)
                    if u == 2:
                        edge_parts(i, u)
                    if first and u == 1:
                        dve.wait_ge(seg_out, 64)
                    if not (first and u == 0):
                        residual_rows(g - 1, (u + 1) % 2)
                    if u < 2:
                        edge_parts(i, u)
                    if last and u == 2:
                        dve.wait_ge(slots_ok, NE)
                        nc.vector.tensor_tensor(h_row[:, :], slots[:, :], base[:, :], ALU.min).then_inc(row_ok, 1)
                    low_h(g, 1)
                    if not (first and u == 0):
                        moments_rows(g - 1, (u + 1) % 2)
                if last:
                    factors_rows(NG - 2, 0)
                    residual_rows(NG - 1, 1)
                    moments_rows(NG - 1, 1)
                    factors_rows(NG - 1, 1)
            passes(dve, body)

            nc.vector.memset(run[:, :, G - 1:G], 0.0).then_inc(c_run_ok, K)

            def scan(j, b, k):
                if k == 0:
                    dve.wait_ge(c_seg_in[b], slot_use(j, b))
                dve.wait_ge(c_hs_ok, j * K + k + 1)
                dve.wait_ge(c_run_ok, j * K + k + 1)
                nc.vector.tensor_tensor_scan(run[:, k], seg_of(b)[:, 0:G], h_full[:, 0, k], run[:, k, G - 1:G], ALU.mult, ALU.add)\
                    .then_inc(c_run_ok, 1)

            def means(j, b):
                dve.wait_ge(c_run_ok, (j + 2) * K)
                after(dve, c_mhi_ok, j)
                nc.vector.tensor_tensor(mean[:, :, :], run[:, :, :], seg_of(b)[:, G:2 * G].unsqueeze(1).to_broadcast([P, K, G]), ALU.mult)\
                    .then_inc(c_mean_ok, 1)

            def low_dst(j, b, k):
                dve.wait_ge(c_hdhi_ok, j * K + k + 1)
                nc.vector.scalar_tensor_tensor(xe_lo[:, b, k], ps_h1[:, k], 0.0, xe_hi[:, b, k].bitcast(f32), ALU.max, ALU.subtract)\
                    .then_inc(c_hdlo_ok, 1)

            def mean_low(j, b):
                dve.wait_ge(c_mhi_ok, j + 1)
                nc.vector.tensor_tensor(xt_lo[:, b], mean[:, :, :], xt_hi[:, b].bitcast(f32), ALU.subtract).then_inc(c_mlo_ok, 1)

            def low_second(j, b, k):
                dve.wait_ge(c_hhi_ok, j * K + k + 1)
                nc.vector.tensor_tensor(h_lo[:, b, k], h_full[:, 1, k], h_hi[:, b, k].bitcast(f32), ALU.subtract).then_inc(c_hlo_ok, 1)

            def residual_edges(j, b):
                dve.wait_ge(c_xb_in[b], slot_use(j, b))
                after(dve, c_o_ok, j - 1)
                residual(j, b, c_l3_ps, c_y_ok)
                sums(j, b, c_y_ok, c_stats_ok)

            def averages_edges(j, b):
                averages(j, b, c_stats_ok, c_mv_ok)

            def factors_edges(j, b):
                factors(j, b, c_sd_ok, c_rs_ok, c_nb_ok)

            for k in range(K):
                scan(0, 0, k)
            means(0, 0)
            for k in range(K):
                low_dst(0, 0, k)
            mean_low(0, 0)

            def step(j, b, left):
                early = isinstance(j, int) and j < 2
                if not early:
                    dve.wait_ge(c_stats_ok, j - 1)
                if left:
                    scan(j + 1, 1 - b, 0)
                if not early:
                    aggregate(b, c_mv_ok)
                if left:
                    scan(j + 1, 1 - b, 1)
                    low_dst(j + 1, 1 - b, 0)
                    means(j + 1, 1 - b)
                    low_dst(j + 1, 1 - b, 1)
                low_second(j, b, 0)
                if not early:
                    factors_edges(j - 2, b)
                if left:
                    mean_low(j + 1, 1 - b)
                low_second(j, b, 1)
                if isinstance(j, int) and j == 0:
                    dve.wait_ge(o_ok, NG)
                else:
                    residual_edges(j - 1, 1 - b)
                if not left:
                    averages_edges(j - 1, 1 - b)
                    factors_edges(j - 1, 1 - b)
                    residual_edges(j, b)
                    averages_edges(j, b)
                    factors_edges(j, b)
            edge_passes(dve, step)

        @block.tensor
        def _(pe):
            def turn(ps, rows_of, k):
                for s in range(S):
                    ins = nc.tensor.transpose(ps[:, k, s * P:(s + 1) * P], rows_of[:, s, k * P:(k + 1) * P], ident[:, :])
                return ins

            def columns(parts, ps, m):
                first = True
                for w, hi, lo in parts:
                    for k in range(K):
                        for wx, a in ((w_hi, hi), (w_lo, hi), (w_hi, lo)):
                            end = k == K - 1 and a is lo and w == parts[-1][0]
                            ins = nc.tensor.matmul(ps[:, m], wx[:, w, k, m * P:(m + 1) * P], a[:, k], start=first, stop=end)
                            first = False
                return ins

            def by_rows(parts, ps, s):
                first = True
                for w, hi, lo in parts:
                    for k in range(K):
                        for a, wx in ((hi, w_hi), (hi, w_lo), (lo, w_hi)):
                            end = k == K - 1 and a is lo and w == parts[-1][0]
                            ins = nc.tensor.matmul(ps[:, s // 2, s % 2 * D:(s % 2 + 1) * D], a[:, k, s * P:(s + 1) * P],
                                                   wx[:, w, k], start=first, stop=end)
                            first = False
                return ins

            def turn_rows(i, u, g):
                pe.wait_ge(x_in[u], 16 * (i + 1))
                for k in range(K):
                    turn(ps_x, xn[:, u], k).then_inc(xt_ps, 1)

            pe.wait_ge(cleared, 3)
            turn_rows(0, 0, 0)
            pe.wait_ge(cleared, 5)
            pe.wait_ge(prep, PREP_IDX)
            for c in range(6):
                ins = nc.tensor.transpose(ps_h2[:, c // S, c % S * P:(c % S + 1) * P], e_idx[:, c // 2, c % 2 * P:(c % 2 + 1) * P], ident[:, :])
            ins.then_inc(turned_pre, 1)
            pe.wait_ge(prep, PREP_ENDS)
            for n in range(2):
                ins = nc.tensor.transpose(ps_y[:, 0, n * P:(n + 1) * P], tr[:, n], ident[:, :])
            ins.then_inc(turned_pre, 1)
            pe.wait_ge(prep, PREP_CARRY)
            nc.tensor.transpose(ps_y[:, 0, 0:P], tr[:, 2], ident[:, :]).then_inc(turned_pre, 1)
            pe.wait_ge(w_ok, 1)

            def last_layer(g, b, low_ok, y_s, l3):
                pe.wait_ge(low_ok, (g + 1) * K)
                for s in range(S):
                    if s % 2 == 0:
                        after(pe, y_s, (g - 1) * K + s // 2 + 1)
                    ins = by_rows([(X3, h_hi[:, b], h_lo[:, b])], ps_y, s)
                    if s % 2:
                        ins.then_inc(l3, 1)

            def edges(i, u):
                xs, xd = (xe_hi[:, 0], xe_lo[:, 0]), (xe_hi[:, 1], xe_lo[:, 1])
                if u == 0:
                    pe.wait_ge(xs_in, 16 * S * (i + 1))
                    for k in range(K):
                        turn(ps_x, xe[:, 0], k).then_inc(xs_ps, 1)
                if u == 1:
                    pe.wait_ge(xd_in, 16 * S * (i + 1))
                    for k in range(K):
                        turn(ps_x, xe[:, 1], k).then_inc(xd_ps, 1)
                if u == 2:
                    pe.wait_ge(xs_ok, i + 1)
                    for s in range(S):
                        ins = by_rows([(X1R, *xs)], ps_x, s)
                        if s % 2:
                            ins.then_inc(src_ps, 1)
                if u == 3:
                    pe.wait_ge(mlo_ok, i + 1)
                    pe.wait_ge(xd_ok, i + 1)
                    for s in range(S):
                        ins = by_rows([(X1R, *xd), (X1L, mean_hi, mean_lo)], ps_x, s)
                        if s % 2:
                            ins.then_inc(dst_ps, 1)

            def ps_x_free(i, u):
                if u == 0:
                    pe.wait_ge(xsf_ok, (i + 1) * K)
                if u == 1:
                    pe.wait_ge(xdf_ok, (i + 1) * K)
                if u == 2:
                    pe.wait_ge(src_ok, (i + 1) * K)
                if u == 3:
                    pe.wait_ge(dst_ok, (i + 1) * K)

            def body(i, first, last):
                for u in range(U):
                    g = i * U + u
                    pe.wait_ge(xlo_ok, (g + 1) * K)
                    after(pe, hf_ok[0], g * K)
                    for m in range(K):
                        columns([(X1R, xt_hi[:, u % 2], xt_lo[:, u % 2])], ps_h1, m).then_inc(l_ps[0], 1)
                    edges(i, u)
                    if not (first and u == 0):
                        last_layer(g - 1, 1, hlo_ok[1], y_ok, l3_ps)
                    if not (last and u == U - 1):
                        ps_x_free(i, u)
                        turn_rows(i + (u + 1) // U, (u + 1) % U, g + 1)
                    if first and u == 0:
                        pe.wait_ge(w_ok, 2)
                        pe.wait_ge(idx_ok, 6)
                        pe.wait_ge(prep, PREP_RDEG)
                    pe.wait_ge(hlo_ok[0], (g + 1) * K)
                    after(pe, hf_ok[1], g * K)
                    for m in range(K):
                        columns([(X2R, h_hi[:, 0], h_lo[:, 0])], ps_h2, m).then_inc(l_ps[1], 1)
                if last:
                    last_layer(NG - 1, 1, hlo_ok[1], y_ok, l3_ps)
            passes(pe, body)
            pe.wait_ge(dst_ok, NE * K)
            pe.wait_ge(hf_ok[1], NG * K)

            def turn_edges(j, b):
                pe.wait_ge(c_hs_in[b], slot_use(j, b, 16 * S))
                after(pe, c_hs_ok, j * K)
                for k in range(K):
                    turn(ps_x, xn[:, b], k).then_inc(c_hs_ps, 1)
                pe.wait_ge(c_hd_in[b], slot_use(j, b))
                after(pe, c_hdlo_ok, j * K)
                for k in range(K):
                    turn(ps_h1, xn[:, 2 + b], k).then_inc(c_hd_ps, 1)

            turn_edges(0, 0)

            def step(j, b, left):
                if left:
                    turn_edges(j + 1, 1 - b)
                if isinstance(j, int) and j == 0:
                    pe.wait_ge(y_ok, NG * K)
                pe.wait_ge(c_mlo_ok, j + 1)
                pe.wait_ge(c_hdlo_ok, (j + 1) * K)
                after(pe, c_hf_ok, j * K)
                for m in range(K):
                    columns([(X2R, xe_hi[:, b], xe_lo[:, b]), (X2L, xt_hi[:, b], xt_lo[:, b])], ps_h2, m).then_inc(c_l2_ps, 1)
                if not (isinstance(j, int) and j == 0):
                    last_layer(j - 1, 1 - b, c_hlo_ok, c_y_ok, c_l3_ps)
                if not left:
                    last_layer(j, b, c_hlo_ok, c_y_ok, c_l3_ps)
            edge_passes(pe, step)


PREP_IDX = 8
PREP_ENDS = 12
PREP_CARRY = 15
PREP_RDEG = 18
_INS = ["x", "src", "dst", "L0_gnn_W1_l", "L0_gnn_b1", "L0_gnn_W1_r", "L0_gnn_W2_l", "L0_gnn_b2",
        "L0_gnn_W2_r", "L0_gnn_W3", "L0_gnn_b3"]
_OUTS = [((100000, 256), "float32")]


def kernel(**inputs):
    import numpy as _np
    import concourse.bacc as _bacc
    from concourse import mybir as _mybir
    from concourse.bass_utils import run_bass_kernel_spmd as _run

    nc = _bacc.Bacc("TRN2", target_bir_lowering=False, num_devices=1)
    arrays, args = {}, []
    for name in _INS:
        a = _np.ascontiguousarray(inputs[name])
        arrays[f"in_{name}_dram"] = a
        args.append(nc.dram_tensor(f"in_{name}_dram", a.shape, _mybir.dt.from_np(a.dtype), kind="ExternalInput").ap())
    for i, (shape, dtype) in enumerate(_OUTS):
        dt = _mybir.dt.from_np(_np.dtype(dtype))
        args.append(nc.dram_tensor(f"out_{i}_dram", shape, dt, kind="ExternalOutput").ap())
    build(nc, *args)
    r = _run(nc, [arrays], core_ids=[0])
    got = tuple(r.results[0][f"out_{i}_dram"] for i in range(len(_OUTS)))
    return got[0]
```
